# Optimizing a Trainium2 kernel written in Bass

```python
import numpy as np
import jax
import jax.numpy as jnp

def _softmax(x, axis=-1):
    return jax.nn.softmax(x, axis=axis)

def _gelu(x):
    return jax.nn.gelu(x, approximate=True)

def _silu(x):
    return jax.nn.silu(x)

def _sigmoid(x):
    return jax.nn.sigmoid(x)

def _layernorm(x, axis=-1, eps=1e-05):
    m = jnp.mean(x, axis=axis, keepdims=True)
    v = jnp.var(x, axis=axis, keepdims=True)
    return (x - m) / jnp.sqrt(v + eps)

def _scatter_add(tgt, idx, src, axis=0):
    return tgt.at[idx].add(src)

def _segment_sum(src, seg, n):
    return jax.ops.segment_sum(src, seg, n)
kernel_name = 'mk_prb_d1_jaxref_r4_48e697'

def setup_inputs(seed: int=0):
    np.random.seed(seed)
    _w = jnp.asarray

    def _L0_attn_setup():
        import jax, jax.numpy as jnp
        import numpy as np
        B, N, D = (4, 1024, 256)
        H, F = (16, 128)
        HD = D // H
        key = jax.random.key(seed)
        k1, k2, k3, k4, k5 = jax.random.split(key, 5)
        x = jax.random.normal(k1, (B, N, D), dtype=jnp.float32)
        W_qkv = jax.random.normal(k2, (3 * D, D), dtype=jnp.float32) * np.sqrt(2.0 / D)
        proj = jax.random.normal(k3, (H, HD, F), dtype=jnp.float32) / np.sqrt(HD)
        W_out = jax.random.normal(k4, (D, D), dtype=jnp.float32) * np.sqrt(2.0 / D)
        b_out = jnp.zeros((D,), dtype=jnp.float32)
        return {'x': x, 'W_qkv': W_qkv, 'proj': proj, 'W_out': W_out, 'b_out': b_out}
    _L0_attn_in = _L0_attn_setup()

    def _L0_ffn_setup():
        import jax, jax.numpy as jnp
        import numpy as np
        from jax import lax
        D = 256
        H = 1024
        E = 8
        TOPK = 2
        key = jax.random.key(seed)
        ks = jax.random.split(key, 7)
        s = 0.02
        return {'x': jax.random.normal(ks[0], (2, 512, D), dtype=jnp.float32), 'W1': jax.random.normal(ks[1], (E, D, H), dtype=jnp.float32) * s, 'b1': jnp.zeros((E, H), dtype=jnp.float32), 'W2': jax.random.normal(ks[2], (E, H, D), dtype=jnp.float32) * s, 'b2': jnp.zeros((E, D), dtype=jnp.float32), 'Wr': jax.random.normal(ks[3], (D, E), dtype=jnp.float32) * s, 'br': jnp.zeros((E,), dtype=jnp.float32)}
    _L0_ffn_in = _L0_ffn_setup()
    _d = {'L0_attn_x': _L0_attn_in['x'], 'L0_attn_W_qkv': _L0_attn_in['W_qkv'], 'L0_attn_proj': _L0_attn_in['proj'], 'L0_attn_W_out': _L0_attn_in['W_out'], 'L0_attn_b_out': _L0_attn_in['b_out'], 'L0_ffn_W1': _L0_ffn_in['W1'], 'L0_ffn_b1': _L0_ffn_in['b1'], 'L0_ffn_W2': _L0_ffn_in['W2'], 'L0_ffn_b2': _L0_ffn_in['b2'], 'L0_ffn_Wr': _L0_ffn_in['Wr'], 'L0_ffn_br': _L0_ffn_in['br']}
    _x0 = _d['L0_attn_x']
    _d['L0_attn_x'] = jax.random.normal(jax.random.fold_in(jax.random.key(seed), 1), (8, 512, 256), dtype=_x0.dtype)
    del _x0
    return _d

def reference(L0_attn_x, L0_attn_W_qkv, L0_attn_proj, L0_attn_W_out, L0_attn_b_out, L0_ffn_W1, L0_ffn_b1, L0_ffn_W2, L0_ffn_b2, L0_ffn_Wr, L0_ffn_br):

    def _L0_attn_ref(x, W_qkv, proj, W_out, b_out):
        import jax, jax.numpy as jnp
        import numpy as np
        B, N, D = (4, 1024, 256)
        H, F = (16, 128)
        HD = D // H
        b, n, d = x.shape
        qkv = x @ W_qkv.T
        q, k, v = jnp.split(qkv, 3, axis=-1)
        reshp = lambda t: t.reshape(b, n, H, HD).transpose(0, 2, 1, 3)
        q, k, v = (reshp(q), reshp(k), reshp(v))
        q_p = jax.nn.elu(jnp.einsum('bhnd,hdf->bhnf', q, proj)) + 1.0
        k_p = jax.nn.elu(jnp.einsum('bhnd,hdf->bhnf', k, proj)) + 1.0
        kv = jnp.einsum('bhnf,bhnd->bhfd', k_p, v)
        attn = jnp.einsum('bhnf,bhfd->bhnd', q_p, kv)
        k_sum = k_p.sum(axis=2)
        z = 1.0 / (jnp.einsum('bhnf,bhf->bhn', q_p, k_sum) + 1e-08)
        attn = attn * z[..., None]
        attn = attn.transpose(0, 2, 1, 3).reshape(b, n, d)
        return attn @ W_out.T + b_out

    def _L0_ffn_ref(x, W1, b1, W2, b2, Wr, br):
        import jax, jax.numpy as jnp
        import numpy as np
        from jax import lax
        D = 256
        H = 1024
        E = 8
        TOPK = 2
        B, S, _ = x.shape
        xf = x.reshape(-1, D)
        logits = xf @ Wr + br
        topv, _ = lax.top_k(logits, TOPK)
        thresh = topv[:, TOPK - 1:TOPK]
        masked = jnp.where(logits >= thresh, logits, -jnp.inf)
        weights = jax.nn.softmax(masked, axis=-1)
        h = jax.nn.gelu(jnp.einsum('td,edh->eth', xf, W1) + b1[:, None, :], approximate=False)
        expert_out = jnp.einsum('eth,ehd->etd', h, W2) + b2[:, None, :]
        out = jnp.einsum('etd,te->td', expert_out, weights)
        return out.reshape(B, S, D)
    x = L0_attn_x
    xn = _layernorm(x, axis=-1)
    x = x + _L0_attn_ref(xn, L0_attn_W_qkv, L0_attn_proj, L0_attn_W_out, L0_attn_b_out) + _L0_ffn_ref(xn, L0_ffn_W1, L0_ffn_b1, L0_ffn_W2, L0_ffn_b2, L0_ffn_Wr, L0_ffn_br)
    return x

_drawn_inputs = setup_inputs


def setup_inputs(seed=0):
    import zlib

    import numpy as np

    out = dict(_drawn_inputs(seed))
    spreads = {'L0_attn_b_out': (0.0, 0.1),
     'L0_ffn_b1': (0.0, 0.319),
     'L0_ffn_b2': (0.0, 0.1),
     'L0_ffn_br': (0.0, 0.1)}
    factors = {'L0_attn_proj': 3.951}
    for name, (base, spread) in spreads.items():
        noise = np.random.default_rng([zlib.crc32(name.encode()), seed]).standard_normal(out[name].shape)
        drawn = base * np.exp(spread * noise) if base else spread * noise
        out[name] = jnp.asarray(drawn.astype(out[name].dtype))
    for name, factor in factors.items():
        out[name] = (out[name] * factor).astype(out[name].dtype)
    return out
```

```python
import concourse.bass as bass
from concourse import mybir

F32 = mybir.dt.float32
F32R = mybir.dt.float32r
BF16 = mybir.dt.bfloat16
I32 = mybir.dt.int32
U32 = mybir.dt.uint32
ACT = mybir.ActivationFunctionType
ALU = mybir.AluOpType
AX_X = mybir.AxisListType.X

P = 128
NB, NTOK, D = 8, 512, 256
TOKENS = NB * NTOK
HEADS, HD, FEAT = 16, 16, 128
KT = D // P
NT = NTOK // P
E, HID = 8, 1024
MT = HID // P
T = 256
SUB = T // P
CAP = TOKENS + T
ROWW = 272
W_COL, TOK_COL = D, D + E
SKIP = E * CAP
EPS = 1e-5
QKVR = 3 * D + E
PAIRS = HEADS // 2
SROWS = 97

C_ID, C_TRI, C_SLOT, C_TOK, C_PAD, C_SEL = 0, 128, 256, 288, 320, 324
C_END = C_SEL + 256


def constants():
    import numpy as np
    c = np.zeros((P, C_END), np.float32)
    p = np.arange(P)
    c[:, C_ID:C_ID + P] = np.eye(P)
    c[:, C_TRI:C_TRI + P] = p[:, None] < p[None, :]
    c[:, C_SLOT:C_SLOT + NT * E] = np.tile(np.arange(E) * CAP - SKIP, NT)
    c[:, C_TOK:C_TOK + NB * NT] = p[:, None] + P * np.arange(NB * NT)
    c[:, C_PAD:C_PAD + SUB] = p[:, None] + P * np.arange(SUB) + TOKENS
    for g in range(2):
        for r in range(P):
            c[32 * (r // 32) + 2 * g + (r % 32) // 16, C_SEL + P * g + r] = 1.0
    return c


def build(nc, x, W_qkv, proj, W_out, b_out, W1, b1, W2, b2, Wr, br, consts, out):
    xg = nc.dram_tensor("xg", (E * CAP, ROWW), F32, kind="Internal").ap()
    acc = nc.dram_tensor("acc", (TOKENS + T, D), F32, kind="Internal").ap()
    x_rows = x.rearrange("b (t p) d -> b p t d", p=P)
    acc_rows = acc[0:TOKENS, :].rearrange("(b t p) d -> b p t d", t=NT, p=P)

    place = [nc.sbuf_base + 63 & ~63]

    def sb_at(name, shape, dt, offset):
        return nc.alloc_sbuf_tensor_at(name, shape, dt, offset=offset)

    def sb(name, shape, dt):
        n = 2 if dt == BF16 else 4
        for s in shape[1:]:
            n *= s
        at = place[0]
        place[0] += (n + 63) // 64 * 64
        assert place[0] <= nc.sbuf_usable_end, (name, place[0])
        return sb_at(name, shape, dt, at)

    cst = sb("cst", [P, C_END], F32)
    ident = cst[:, C_ID:C_ID + P]
    tri = sb("tri", [P, P], BF16)
    ones = sb("ones", [P, P], BF16)
    zrows = sb("zrows", [P, SUB, ROWW], F32)
    b1T = sb("b1T", [P, E * MT], F32)
    b2bc = sb("b2bc", [P, E * D], F32)
    counts = sb("counts", [1, 8, 16], F32)
    counts_i = sb("counts_i", [1, 4, 16], I32)
    WTh = sb("WTh", [P, KT, QKVR], F32R)
    WTl = sb("WTl", [P, KT, QKVR], F32R)
    WOh = sb("WOh", [P, KT, D], F32R)
    WOl = sb("WOl", [P, KT, D], F32R)
    stacked_proj = sb("stacked_proj", [P, HEADS, FEAT], F32R)
    br_bc = sb("br_bc", [P, NT, E], F32)
    bo_bc = sb("bo_bc", [P, D], F32)
    xin = sb("xin", [P, NT, D], F32)
    xres = sb("xres", [P, NT, D], F32)
    xn = sb("xn", [P, NT, D], F32)
    rows = sb("rows", [P, NT, ROWW], F32)
    stats = sb("stats", [P, NT, 6], F32)
    mv = sb("mv", [P, NT, 2], F32)
    tokens = sb("tokens", [P, NT], F32)
    var = sb("var", [P, NT], F32)
    rs = sb("rs", [P, 2, NT], F32)
    rtmp = sb("rtmp", [P, 2, NT], F32)
    rbits = sb("rbits", [P, NT], I32)
    lraw = sb("lraw", [P, NT, E], F32)
    lg = sb("lg", [P, NT, E], F32)
    top8 = sb("top8", [P, NT, 8], F32)
    msk = sb("msk", [P, NT, E], F32)
    mskb = sb("mskb", [P, NT, E], BF16)
    dlt = sb("dlt", [P, NT, E], F32)
    ex = sb("ex", [P, NT, E], F32)
    exm = sb("exm", [P, NT, E], F32)
    esum = sb("esum", [P, NT], F32)
    erec = sb("erec", [P, NT], F32)
    cum = sb("cum", [P, NT + 1, E], F32)
    cumb = sb("cumb", [P, NT, E], BF16)
    totb = sb("totb", [P, E], BF16)
    slotf = sb("slotf", [P, 2, NT * E], F32)
    slots = sb("slots", [P, NT * E], U32)
    e_ring = sb("e_ring", [P, 4, 512], F32)
    kv_sb = sb("kv_sb", [P, 512], F32)
    num_w = sb("num_w", [P, HEADS, 32], F32)
    den_w = sb("den_w", [P, HEADS, 32], F32)
    r_num = place[0]
    num_sb = sb("num_sb", [P, 2, 512], F32)
    den_sb = sb("den_sb", [P, 512], F32)
    rec_sb = sb("rec_sb", [P, 512], F32)
    at = sb("at", [P, 2, 512], F32)
    ath = sb("ath", [P, 2, 512], F32R)
    atl = sb("atl", [P, 2, 512], F32R)
    o_sb = sb("o_sb", [P, NT, D], F32)
    r_qp = place[0]
    qp = sb("qp", [P, HEADS, 512], F32)
    r_kp = place[0]
    kp = sb("kp", [P, 2, 2048], F32)
    vext = sb("vext", [P, NT, HEADS, 32], F32)
    kdh = sb("kdh", [P, 2, 512], F32R)
    kdl = sb("kdl", [P, 2, 512], F32R)
    r_xt = place[0]
    xTh = sb("xTh", [P, KT, 512], F32R)
    xTl = sb("xTl", [P, KT, 512], F32R)
    r_sk = place[0]
    Sk = sb("Sk", [P, PAIRS, 512], F32R)
    r_qd = place[0]
    qdh = sb("qdh", [P, 2, 512], F32R)
    qdl = sb("qdl", [P, 2, 512], F32R)
    Sq = sb("Sq", [P, PAIRS, 512], F32R)
    wnat = sb_at("wnat", [P, 8, D], F32, r_qp)
    wr_nat = sb_at("wr_nat", [P, KT, E], F32, r_qp + 8192)
    b1nat = sb_at("b1nat", [E * MT, P], F32, r_qp + 8320)
    praw = sb_at("praw", [P, HEADS, FEAT], F32, r_qp + 9216)
    phi = sb_at("phi", [P, HEADS, FEAT], F32R, r_qp + 17408)
    KB = 1024
    wh = [sb_at("wh0", [P, 4096], F32R, r_kp), sb_at("wh1", [P, 4096], F32R, r_qp)]
    wl = [sb_at("wl0", [P, 4096], F32R, r_kp + 16 * KB), sb_at("wl1", [P, 4096], F32R, r_qp + 16 * KB)]
    wraw = sb_at("wraw", [P, 4096], F32, r_sk)
    gxh = sb_at("gxh", [P, KT, T], F32R, r_xt)
    gxl = sb_at("gxl", [P, KT, T], F32R, r_xt + 2 * KB)
    grow = sb_at("grow", [P, SUB, ROWW], F32, r_xt + 4 * KB)
    h32 = sb_at("h32", [P, MT, T], F32, r_qd)
    hh = sb_at("hh", [P, MT, T], F32R, r_qd + 8 * KB)
    hl = sb_at("hl", [P, MT, T], F32R, r_qd + 16 * KB)
    assert r_xt - r_kp >= 32 * KB and r_sk - r_xt >= 4 * KB + SUB * ROWW * 4 and r_qd - r_sk >= 16 * KB
    place[0] = r_xt + 4 * KB + SUB * ROWW * 4
    b1c = sb("b1c", [P, 2, MT], F32)
    wnext = sb("wnext", [P, SUB, E], F32)
    wcur = sb("wcur", [P, SUB, 1], F32)
    inext = sb("inext", [P, SUB], U32)
    icur = sb("icur", [P, SUB, 1], U32)
    assert place[0] <= r_sk
    ytmp = sb_at("ytmp", [P, SUB, D], F32, r_num)
    ysb = sb_at("ysb", [P, SUB, D], F32, r_num + 2 * KB)

    def bank(name):
        return nc.alloc_psum_tensor(name, [P, 512], F32)

    F = [bank(f"F{i}") for i in range(4)]
    WK = [bank(f"WK{i}") for i in range(2)]
    NUM, DEN = bank("NUM"), bank("DEN")
    KV = DEN

    sem = nc.alloc_semaphore
    s_w = sem("s_w")
    s_zero = sem("s_zero")
    s_praw = sem("s_praw")
    s_wT = sem("s_wT")
    s_wTh = sem("s_wTh")
    s_setup = sem("s_setup")
    x_ld = sem("x_ld")
    xres_ld = sem("xres_ld")
    xn_rdy = sem("xn_rdy")
    xT_full = sem("xT_full")
    qk_full = sem("qk_full")
    v_full = sem("v_full")
    pos_full = sem("pos_full")
    pos_read = sem("pos_read")
    state_full = sem("state_full")
    spread_full = sem("spread_full")
    proj_full = sem("proj_full")
    f_full = sem("f_full")
    relu_done = sem("relu_done")
    exp_done = sem("exp_done")
    feat = sem("feat")
    kv_done = sem("kv_done")
    kv_rdy = sem("kv_rdy")
    state_rdy = sem("state_rdy")
    attn_done = sem("attn_done")
    num_rdy = sem("num_rdy")
    den_read = sem("den_read")
    rec_rdy = sem("rec_rdy")
    at_rdy = sem("at_rdy")
    ath_rdy = sem("ath_rdy")
    atl_rdy = sem("atl_rdy")
    xth_rdy = sem("xth_rdy")
    xtl_rdy = sem("xtl_rdy")
    qkh_rdy = sem("qkh_rdy")
    qkl_rdy = sem("qkl_rdy")
    sk_ld = sem("sk_ld")
    sq_ld = sem("sq_ld")
    lraw_rdy = sem("lraw_rdy")
    v_rdy = sem("v_rdy")
    dlt_rdy = sem("dlt_rdy")
    ex_rdy = sem("ex_rdy")
    mask_rdy = sem("mask_rdy")
    rows_rdy = sem("rows_rdy")
    slot_rdy = sem("slot_rdy")
    sent = sem("sent")
    xres_rdy = sem("xres_rdy")
    o_rdy = sem("o_rdy")
    acc_st = sem("acc_st")
    tot_rdy = sem("tot_rdy")
    route_rdy = sem("route_rdy")
    step = sem("step")
    pad_st = sem("pad_st")
    raw_ld = sem("raw_ld")
    w_rdy = sem("w_rdy")
    grow_ld = sem("grow_ld")
    grow_free = sem("grow_free")
    gx_full = sem("gx_full")
    gxh_rdy = sem("gxh_rdy")
    h_full = sem("h_full")
    gelu = sem("gelu")
    hh_rdy = sem("hh_rdy")
    hl_rdy = sem("hl_rdy")
    y_full = sem("y_full")
    y_read = sem("y_read")
    y_rdy = sem("y_rdy")
    added = sem("added")
    sums = sem("sums")
    gx_cur = sem("gx_cur")
    out_st = sem("out_st")

    SETUP_DMAS = 9
    PRAW_DMAS = 6
    STACK_INC = 16 * 12
    SENT_INC = 16 * NT * E
    def wait(eng, s, n):
        if not isinstance(n, int) or n > 0:
            eng.wait_ge(s, n)

    block_ctx = nc.Block()
    block = block_ctx.__enter__()

    @block.sync
    def _(sp):
        sp.dma_start(wnat[:, 0:6, :], W_qkv.rearrange("(c p) d -> p c d", p=P)).then_inc(s_w, 16)
        sp.dma_start(cst[:, :], consts).then_inc(s_w, 16)
        sp.dma_start(xin[:, :, :], x_rows[0]).then_inc(x_ld, 16)
        sp.dma_start(wnat[:, 6:8, :], W_out.rearrange("(c p) d -> p c d", p=P)).then_inc(s_w, 16)
        sp.dma_start(wr_nat[:, :, :], Wr.rearrange("(k p) e -> p k e", p=P)).then_inc(s_w, 16)
        sp.dma_start(b1nat[:, :], b1.rearrange("e (m p) -> (e m) p", p=P)).then_inc(s_w, 16)
        for n in range(NT):
            sp.dma_start(br_bc[:, n, :], br.partition_broadcast(P)).then_inc(s_w, 16)
        sp.wait_ge(s_zero, 1)
        for s in range(2):
            for part in range(3):
                r = 32 * part + 16 * s
                sp.dma_start(praw[r:r + HD, s:HEADS:2, :],
                             proj.rearrange("(i s) d f -> s d i f", s=2)[s]).then_inc(s_praw, 16)
        sp.dma_start(bo_bc[:, :], b_out.partition_broadcast(P)).then_inc(xres_ld, 16)
        sp.dma_start(b2bc[:, :], b2.rearrange("e d -> (e d)").partition_broadcast(P)).then_inc(pad_st, 16)

        def load_x(b):
            wait(sp, xn_rdy, b)
            sp.dma_start(xin[:, :, :], x_rows[b]).then_inc(x_ld, 16)

        def load_xres(b):
            wait(sp, o_rdy, 2 * b)
            sp.dma_start(xres[:, :, :], x_rows[b]).then_inc(xres_ld, 16)

        def stack(dst, hi, lo, done):
            for r in range(4):
                for part, src in enumerate((hi, lo, hi)):
                    sp.dma_start(dst[32 * part:32 * part + 32, r:PAIRS:4, :].bitcast(F32),
                                 src[32 * r:32 * r + 32, :, :].bitcast(F32)).then_inc(done, 16)

        def stack_k(b):
            sp.wait_ge(qkl_rdy, 4 * b + 2)
            wait(sp, f_full, 32 * b - 16)
            stack(Sk, kdh, kdl, sk_ld)

        def stack_q(b):
            sp.wait_ge(qkl_rdy, 4 * b + 4)
            wait(sp, f_full, 32 * b)
            stack(Sq, qdh, qdl, sq_ld)

        def store_o(b):
            sp.wait_ge(o_rdy, 2 * b + 2)
            sp.dma_start(acc_rows[b], o_sb[:, :, :]).then_inc(acc_st, 16)

        load_x(1)
        sp.wait_ge(s_setup, 1)
        stack_k(0)
        stack_q(0)
        load_xres(0)
        load_x(2)
        stack_k(1)
        stack_q(1)
        with sp.Fori(1, NB - 2) as b:
            store_o(b - 1)
            load_xres(b)
            load_x(b + 2)
            stack_k(b + 1)
            stack_q(b + 1)
        store_o(NB - 3)
        load_xres(NB - 2)
        stack_k(NB - 1)
        stack_q(NB - 1)
        store_o(NB - 2)
        load_xres(NB - 1)
        def load_raw(e):
            sp.dma_start(wraw[:, 0:2048], W1[e].rearrange("(k p) h -> p k h", p=P)).then_inc(raw_ld, 16)
            sp.dma_start(wraw[:, 2048:4096], W2[e].rearrange("(m p) d -> p m d", p=P)).then_inc(raw_ld, 16)

        sp.wait_ge(f_full, 32 * NB - 16)
        load_raw(0)
        sp.wait_ge(route_rdy, 1)
        for e in range(E):
            n = sp.value_load(counts_i[0:1, 0, e:e + 1], min_val=0, max_val=TOKENS)
            sp.dma_start(xg[bass.ds(n + e * CAP, T), :].rearrange("(s p) c -> p s c", p=P),
                         zrows[:, :, :]).then_inc(pad_st, 16)
        sp.dma_start(acc[TOKENS:TOKENS + T, :].rearrange("(s p) c -> p s c", p=P),
                     zrows[:, :, 0:D]).then_inc(pad_st, 16)
        store_o(NB - 1)
        sp.wait_ge(pad_st, 16 * (E + 2))
        sp.wait_ge(sent, SENT_INC * NB)

        def load_rows(g, first):
            sp.wait_ge(grow_free, g + 1)
            sp.dma_start(grow[:, :, :],
                         xg[bass.ds(first, T), :].rearrange("(s p) c -> p s c", p=P)).then_inc(grow_ld, 16)

        def expert_rows(e):
            lo = sp.value_load(counts_i[0:1, 1, bass.ds(e, 1)], min_val=0, max_val=E * TOKENS // T)
            hi = sp.value_load(counts_i[0:1, 1, bass.ds(e + 1, 1)], min_val=1, max_val=E * TOKENS // T)
            with sp.Fori(lo, hi) as g:
                load_rows(g, nc.s_assert_within((g - lo) * T + e * CAP, 0, E * CAP - T,
                                                skip_runtime_bounds_check_because="a list has at most TOKENS rows"))

        sp.wait_ge(w_rdy, 1)
        load_raw(1)
        with sp.Fori(0, E // 2 - 1) as i:
            for s in range(2):
                expert_rows(2 * i + s)
                sp.wait_ge(w_rdy, 2 * i + s + 2)
                load_raw(2 * i + s + 2)
        expert_rows(E - 2)
        expert_rows(E - 1)
        total = sp.value_load(counts_i[0:1, 1, E:E + 1], min_val=E, max_val=E * TOKENS // T)
        load_rows(total, 0)
        sp.wait_ge(sums, SUB + SUB * total)
        for q in range(4):
            n = TOKENS // 4
            sp.dma_start(out.rearrange("b t d -> (b t) d")[q * n:q * n + n, :],
                         acc[q * n:q * n + n, :]).then_inc(out_st, 16)
        sp.wait_ge(out_st, 64)

    @block.tensor
    def _(pe):
        def mm3(dst, wh_, wl_, mh_, ml_, first, last):
            nc.tensor.matmul(dst, wh_, mh_, start=first, stop=False)
            nc.tensor.matmul(dst, wh_, ml_, start=False, stop=False)
            return nc.tensor.matmul(dst, wl_, mh_, start=False, stop=last)

        pe.wait_ge(s_w, 16 * SETUP_DMAS)
        for k in range(KT):
            for c in range(6):
                t = 6 * k + c
                last = nc.tensor.transpose(F[t // 4][:, t % 4 * P:(t % 4 + 1) * P],
                                           wnat[:, c, k * P:(k + 1) * P], ident)
        last.then_inc(s_wT, 1)
        for k in range(KT):
            for c in range(2):
                last = nc.tensor.transpose(F[3][:, k * D + c * P:k * D + (c + 1) * P],
                                           wnat[:, 6 + c, k * P:(k + 1) * P], ident)
        last.then_inc(s_wT, 1)
        nc.tensor.transpose(NUM[:, 0:E * MT], b1nat[:, :], cst[0:E * MT, C_ID:C_ID + E * MT]).then_inc(s_wT, 1)

        def stage_a(b, bank_waits):
            pe.wait_ge(xn_rdy, b + 1)
            for k in range(KT):
                for sem_, n_ in bank_waits[k]:
                    pe.wait_ge(sem_, n_)
                for n in range(NT):
                    last = nc.tensor.transpose(WK[k][:, n * P:(n + 1) * P], xn[:, n, k * P:(k + 1) * P], ident)
                last.then_inc(xT_full, 1)
            pe.wait_ge(xtl_rdy, 2 * b + 2)
            for i, (bk, col) in enumerate(((1, D), (0, D + P), (1, 0), (0, P))):
                if i >= 2:
                    pe.wait_ge(qkl_rdy, 4 * b + i - 1)
                for k in range(KT):
                    last = mm3(WK[bk][:, :], WTh[:, k, col:col + P], WTl[:, k, col:col + P],
                               xTh[:, k, :], xTl[:, k, :], k == 0, k == KT - 1)
                last.then_inc(qk_full, 1)
            for n in range(NT):
                if n < 2:
                    pe.wait_ge(qkl_rdy, 4 * b + 3 + n)
                else:
                    pe.wait_ge(v_rdy, NT * b + n - 1)
                for k in range(KT):
                    tok = slice(n * P, (n + 1) * P)
                    last = mm3(WK[1 - n % 2][:, 0:D + E], xTh[:, k, tok], xTl[:, k, tok],
                               WTh[:, k, 2 * D:QKVR], WTl[:, k, 2 * D:QKVR], k == 0, k == KT - 1)
                last.then_inc(v_full, 1)

        def prefix(b):
            pe.wait_ge(mask_rdy, b + 1)
            pe.wait_ge(v_rdy, NT * b + 3)
            nc.tensor.matmul(WK[1][:, 0:NT * E], tri[:, :], mskb[:, :, :], start=True, stop=False)
            nc.tensor.matmul(WK[1][:, 0:NT * E], ones[:, :], cumb[:, :, :],
                             start=False, stop=True).then_inc(pos_full, 1)

        def k_units(b, n):
            for c in range(4):
                f = 32 * b + 4 * n + c
                wait(pe, feat, f - 3)
                for s in range(2):
                    pr = 2 * c + s
                    last = nc.tensor.matmul(F[c][:, s * D:(s + 1) * D], Sk[0:SROWS, pr, n * P:(n + 1) * P],
                                            stacked_proj[0:SROWS, 2 * pr:2 * pr + 2, :], start=True, stop=True)
                last.then_inc(f_full, 1)

        def kv(b, n):
            pe.wait_ge(feat, 32 * b + 4 * n + 4)
            if n == 0:
                pe.wait_ge(v_rdy, NT * b + NT)
                wait(pe, den_read, b)
            for c in range(4):
                for j in range(4):
                    h = 4 * c + j
                    last = nc.tensor.matmul(KV[32 * j:32 * j + 32, c * P:(c + 1) * P], vext[:, n, h, :],
                                            kp[:, n % 2, h * FEAT:(h + 1) * FEAT],
                                            start=n == 0 and c == 0, stop=n == NT - 1, skip_group_check=True)
            last.then_inc(kv_done, 1)

        def state_T(b, sem_, n_):
            pe.wait_ge(kv_rdy, b + 1)
            pe.wait_ge(sem_, n_)
            for c in range(4):
                last = nc.tensor.transpose(WK[0][:, c * P:(c + 1) * P], kv_sb[:, c * P:(c + 1) * P], ident)
            last.then_inc(state_full, 1)

        def q_units(b, lo, hi):
            for h in range(lo, hi):
                wait(pe, feat, 32 * b + 16 + h - 3)
                nc.tensor.matmul(F[h % 4][:, :], stacked_proj[0:SROWS, h, :], Sq[0:SROWS, h // 2, :],
                                 start=True, stop=True).then_inc(f_full, 1)

        def attn(b, g):
            pe.wait_ge(feat, 32 * b + 16 + 8 * (g + 1))
            if g == 0:
                pe.wait_ge(state_rdy, b + 1)
            wait(pe, num_rdy, 2 * b + g)
            for s in range(2):
                for j in range(4):
                    h = 8 * g + 2 * j + s
                    nc.tensor.matmul(NUM[32 * j:32 * j + 32, :], num_w[:, h, :], qp[:, h, :],
                                     start=s == 0, stop=s == 1)
                for j in range(4):
                    h = 8 * g + 2 * j + s
                    last = nc.tensor.matmul(DEN[32 * j:32 * j + 32, :], den_w[:, h, :], qp[:, h, :],
                                            start=g == 0 and s == 0, stop=g == 1 and s == 1,
                                            skip_group_check=True)
            last.then_inc(attn_done, 1)

        def spread(b):
            pe.wait_ge(rec_rdy, b + 1)
            pe.wait_ge(state_rdy, b + 1)
            pe.wait_ge(pos_read, b + 2)
            for g in range(2):
                nc.tensor.matmul(WK[g][:, :], cst[:, C_SEL + P * g:C_SEL + P * (g + 1)], rec_sb[:, :],
                                 start=True, stop=True).then_inc(spread_full, 1)

        def project(b):
            pe.wait_ge(atl_rdy, 2 * b + 2)
            for i in range(2):
                for n in range(2):
                    tok = slice((2 * i + n) * P, (2 * i + n + 1) * P)
                    for g in range(2):
                        last = mm3(WK[i][:, n * D:(n + 1) * D], ath[:, g, tok], atl[:, g, tok],
                                   WOh[:, g, :], WOl[:, g, :], g == 0, g == 1)
                last.then_inc(proj_full, 1)

        def iteration(b, first=False, last=False):
            pe.wait_ge(sk_ld, STACK_INC * (b + 1))
            k_units(b, 0)
            k_units(b, 1)
            kv(b, 0)
            k_units(b, 2)
            kv(b, 1)
            if not first:
                spread(b - 1)
            k_units(b, 3)
            kv(b, 2)
            if not first:
                project(b - 1)
            kv(b, 3)
            if first:
                stage_a(b + 1, [[(v_rdy, NT)], [(pos_read, 1)]])
            elif not last:
                stage_a(b + 1, [[(o_rdy, 2 * b - 1)], [(o_rdy, 2 * b)]])
            if not last:
                state_T(b, v_rdy, NT * b + 2 * NT)
            else:
                state_T(b, o_rdy, 2 * b - 1)
            pe.wait_ge(sq_ld, STACK_INC * (b + 1))
            q_units(b, 0, 8)
            if not last:
                prefix(b + 1)
            else:
                pe.wait_ge(tot_rdy, 1)
                pe.wait_ge(o_rdy, 2 * b)
                nc.tensor.matmul(WK[1][:, 0:E], ones[:, :], totb[:, :], start=True, stop=True).then_inc(pos_full, 1)
            q_units(b, 8, 12)
            attn(b, 0)
            q_units(b, 12, 16)
            attn(b, 1)

        pe.wait_ge(s_setup, 1)
        stage_a(0, [[], []])
        prefix(0)
        iteration(0, first=True)
        with pe.Fori(1, NB - 1) as b:
            iteration(b)
        iteration(NB - 1, last=True)
        spread(NB - 1)
        project(NB - 1)

        def rows_T(g):
            pe.wait_ge(grow_ld, 16 * g + 16)
            pe.wait_ge(grow_free, g + 1)
            for k in range(KT):
                for s in range(SUB):
                    last = nc.tensor.transpose(WK[0][:, k * T + s * P:k * T + (s + 1) * P],
                                               grow[:, s, k * P:(k + 1) * P], ident)
            last.then_inc(gx_full, 1)

        def tile(g, w):
            w1 = [wh[w][:, 0:2048].rearrange("p (k h) -> p k h", k=KT), wl[w][:, 0:2048].rearrange("p (k h) -> p k h", k=KT)]
            w2 = [wh[w][:, 2048:4096].rearrange("p (m d) -> p m d", m=MT), wl[w][:, 2048:4096].rearrange("p (m d) -> p m d", m=MT)]
            pe.wait_ge(grow_free, g + 2)
            for m in range(MT):
                pe.wait_ge(gelu, MT * g + m + 1)
                for k in range(KT):
                    hid = slice(m * P, (m + 1) * P)
                    last = mm3(F[m % 4][:, 0:T], w1[0][:, k, hid], w1[1][:, k, hid],
                               gxh[:, k, :], gxl[:, k, :], k == 0, k == KT - 1)
                last.then_inc(h_full, 1)
            rows_T(g + 1)
            for s in range(SUB):
                pe.wait_ge(y_read, SUB * g + s + 1)
                row = slice(s * P, (s + 1) * P)
                for m in range(MT):
                    if s == 0 and m % 2 == 0:
                        pe.wait_ge(hl_rdy, 4 + 4 * g + m // 2 + 1)
                    last = mm3((NUM, DEN)[s][:, 0:D], hh[:, m, row], hl[:, m, row],
                               w2[0][:, m, :], w2[1][:, m, :], m == 0, m == MT - 1)
                last.then_inc(y_full, 1)

        pe.sem_inc(y_full, SUB)
        pe.wait_ge(route_rdy, 1)
        pe.wait_ge(feat, 32 * NB)
        pe.wait_ge(num_rdy, 2 * NB)
        pe.wait_ge(den_read, NB)
        pe.wait_ge(o_rdy, 2 * NB)
        rows_T(0)
        with pe.Fori(0, E // 2) as i:
            for s in range(2):
                lo = pe.value_load(counts_i[0:1, 1, bass.ds(2 * i + s, 1)], min_val=0, max_val=E * TOKENS // T)
                hi = pe.value_load(counts_i[0:1, 1, bass.ds(2 * i + s + 1, 1)], min_val=1, max_val=E * TOKENS // T)
                with pe.Fori(lo, hi) as g:
                    pe.wait_ge(w_rdy, 2 * i + s + 1)
                    tile(g, s)

    @block.scalar
    def _(act):
        A = nc.scalar.activation
        act.wait_ge(s_wT, 1)
        for k in range(KT):
            for c in range(6):
                t = 6 * k + c
                last = A(WTh[:, k, c * P:(c + 1) * P], F[t // 4][:, t % 4 * P:(t % 4 + 1) * P], ACT.Copy)
        last = A(WTh[:, :, 3 * D:QKVR], wr_nat[:, :, :], ACT.Copy)
        act.wait_ge(s_wT, 2)
        A(WOh[:, :, :], F[3][:, :].rearrange("p (k d) -> p k d", k=KT), ACT.Copy).then_inc(s_wTh, 1)
        act.wait_ge(s_praw, 16 * PRAW_DMAS)
        A(phi[64:96, :, :], praw[64:96, :, :], ACT.Copy).then_inc(s_wTh, 1)

        def stage_a(b):
            for k in range(KT):
                act.wait_ge(xT_full, 2 * b + k + 1)
                A(xTh[:, k, :], WK[k][:, :], ACT.Copy).then_inc(xth_rdy, 1)
            for i, (bk, dst, g) in enumerate(((1, kdh, 0), (0, kdh, 1), (1, qdh, 0), (0, qdh, 1))):
                act.wait_ge(qk_full, 4 * b + i + 1)
                if g == 0:
                    wait(act, (sk_ld, sq_ld)[i // 2], STACK_INC * b)
                A(dst[:, g, :], WK[bk][:, :], ACT.Copy).then_inc(qkh_rdy, 1)
            wait(act, dlt_rdy, b)
            for n in range(NT):
                act.wait_ge(v_full, NT * b + n + 1)
                A(lraw[:, n, :], WK[1 - n % 2][:, D:D + E], ACT.Copy).then_inc(lraw_rdy, 1)
                A(vext[:, n, :, 0:HD], WK[1 - n % 2][:, 0:D].rearrange("p (h d) -> p h d", d=HD),
                  ACT.Copy).then_inc(v_rdy, 1)

        def route(b):
            act.wait_ge(dlt_rdy, b + 1)
            A(ex[:, :, :], dlt[:, :, :], ACT.Exp).then_inc(ex_rdy, 1)

        def send_rows(b):
            wait(act, sent, SENT_INC * b)
            A(rows[:, :, 0:D], xn[:, :, :], ACT.Copy).then_inc(rows_rdy, 1)

        def exps(b, lo, hi):
            for u in range(lo, hi + 1):
                f = 32 * b + u
                if u < hi:
                    act.wait_ge(f_full, f + 1)
                    wait(act, feat, f - 3)
                    A(e_ring[:, u % 4, :], F[u % 4][:, :], ACT.Relu, bias=1.0, scale=-1.0).then_inc(relu_done, 1)
                if u > lo:
                    act.wait_ge(relu_done, f)
                    A(e_ring[:, (u - 1) % 4, :], e_ring[:, (u - 1) % 4, :], ACT.Exp, scale=-1.0).then_inc(exp_done, 1)

        def at_hi(b):
            for g in range(2):
                act.wait_ge(at_rdy, 2 * b + g + 1)
                A(ath[:, g, :], at[:, g, :], ACT.Copy).then_inc(ath_rdy, 1)

        def copy_num(b, g):
            act.wait_ge(attn_done, 2 * b + g + 1)
            wait(act, at_rdy, 2 * (b - 1) + g + 1)
            A(num_sb[:, g, :], NUM[:, :], ACT.Copy).then_inc(num_rdy, 1)

        def state(b):
            act.wait_ge(state_full, b + 1)
            wait(act, attn_done, 2 * b)
            st = WK[0][:, :].rearrange("p (h c) -> p h c", c=32)
            for s in range(2):
                last = A(num_w[:, s:HEADS:2, 16 * s:16 * s + HD], st[:, s:HEADS:2, 0:HD], ACT.Copy)
            for g in range(2):
                for s in range(2):
                    last = A(den_w[:, 8 * g + s:8 * g + 8:2, 2 * g + s:2 * g + s + 1],
                             st[:, 8 * g + s:8 * g + 8:2, HD:HD + 1], ACT.Copy)
            last.then_inc(state_rdy, 1)

        def iteration(b, first=False, last=False):
            exps(b, 0, 12)
            if not first:
                at_hi(b - 1)
            exps(b, 12, 16)
            act.wait_ge(kv_done, NT * b + NT)
            A(kv_sb[:, :], KV[:, :], ACT.Copy).then_inc(kv_rdy, 1)
            if not last:
                stage_a(b + 1)
            state(b)
            exps(b, 16, 20)
            if not last:
                route(b + 1)
            exps(b, 20, 24)
            if not last:
                send_rows(b + 1)
            exps(b, 24, 28)
            copy_num(b, 0)
            exps(b, 28, 32)
            copy_num(b, 1)

        act.wait_ge(s_setup, 1)
        stage_a(0)
        route(0)
        send_rows(0)
        iteration(0, first=True)
        with act.Fori(1, NB - 1) as b:
            iteration(b)
        iteration(NB - 1, last=True)
        at_hi(NB - 1)

        def rows_hi(g):
            act.wait_ge(gx_full, g + 1)
            A(gxh[:, :, :], WK[0][:, :].rearrange("p (k t) -> p k t", k=KT), ACT.Copy).then_inc(gxh_rdy, 1)

        def tile(g, w):
            for m in range(MT):
                act.wait_ge(h_full, MT * g + m + 1)
                if m % 2 == 0:
                    act.wait_ge(hl_rdy, 4 * g + m // 2 + 1)
                A(h32[:, m, :], F[m % 4][:, 0:T], ACT.Gelu, bias=b1c[:, w, m:m + 1]).then_inc(gelu, 1)
                if m % 2 == 1:
                    if m == 1:
                        act.wait_ge(y_full, SUB * g + SUB)
                    act.wait_ge(gelu, 4 + MT * g + m + 1)
                    A(hh[:, m - 1:m + 1, :], h32[:, m - 1:m + 1, :], ACT.Copy).then_inc(hh_rdy, 1)
            rows_hi(g + 1)

        act.sem_inc(gelu, 4)
        act.wait_ge(route_rdy, 1)
        rows_hi(0)
        with act.Fori(0, E // 2) as i:
            for s in range(2):
                lo = act.value_load(counts_i[0:1, 1, bass.ds(2 * i + s, 1)], min_val=0, max_val=E * TOKENS // T)
                hi = act.value_load(counts_i[0:1, 1, bass.ds(2 * i + s + 1, 1)], min_val=1, max_val=E * TOKENS // T)
                with act.Fori(lo, hi) as g:
                    act.wait_ge(w_rdy, 2 * i + s + 1)
                    tile(g, s)

    @block.vector
    def _(dve):
        V = nc.vector
        chain = [0, 0]

        def link(ins):
            ins.then_inc(step, 1)
            chain[1] += 1
            dve.wait_ge(step, chain[0] + chain[1])

        def f32(t):
            return t.bitcast(F32)

        V.memset(praw[:, :, :], 0.0).then_inc(s_zero, 1)
        V.memset(Sk[96:97, :, :].bitcast(F32), 1.0)
        V.memset(Sq[96:97, :, :].bitcast(F32), 1.0)
        V.memset(vext[:, :, :, HD:32], 1.0)
        V.memset(num_w[:, :, :], 0.0)
        V.memset(den_w[:, :, :], 0.0)
        V.memset(cum[:, :, :], 0.0)
        V.memset(rows[:, :, TOK_COL:ROWW], 0.0)
        link(V.memset(zrows[:, :, :], 0.0))
        V.memset(ones[:, :], 1.0)
        link(V.memset(counts[:, :, :], 0.0))
        dve.wait_ge(s_praw, 16 * PRAW_DMAS)
        link(V.memset(praw[96:97, :, :], 1.0))
        dve.wait_ge(s_w, 16 * SETUP_DMAS)
        V.tensor_copy(tri[:, :], cst[:, C_TRI:C_TRI + P])
        V.tensor_copy(zrows[:, :, TOK_COL], cst[:, C_PAD:C_PAD + SUB])
        dve.wait_ge(s_wT, 3)
        V.tensor_copy(b1T[:, :], NUM[:, 0:E * MT])
        dve.wait_ge(s_wTh, 1)
        for k in range(KT):
            for c in range(6):
                t = 6 * k + c
                V.tensor_tensor(WTl[:, k, c * P:(c + 1) * P], F[t // 4][:, t % 4 * P:(t % 4 + 1) * P],
                                f32(WTh[:, k, c * P:(c + 1) * P]), ALU.subtract)
        V.tensor_tensor(WTl[:, :, 3 * D:QKVR], wr_nat[:, :, :], f32(WTh[:, :, 3 * D:QKVR]), ALU.subtract)
        V.tensor_tensor(WOl[:, :, :], F[3][:, :].rearrange("p (k d) -> p k d", k=KT), f32(WOh[:, :, :]), ALU.subtract)
        dve.wait_ge(s_wTh, 2)
        V.tensor_copy(stacked_proj[0:64, :, :], praw[0:64, :, :])
        V.tensor_tensor(stacked_proj[64:96, :, :], praw[64:96, :, :], f32(phi[64:96, :, :]), ALU.subtract)
        V.tensor_copy(stacked_proj[96:97, :, :], praw[96:97, :, :]).then_inc(s_setup, 1)
        setup_steps = chain[1]

        def norm(b):
            dve.wait_ge(x_ld, 16 * b + 16)
            for n in range(NT):
                last = V.bn_stats(stats[:, n, :], xin[:, n, :])
            link(last)
            V.tensor_copy(tokens[:, :], cst[:, bass.ds(C_TOK + NT * b, NT)])
            for n in range(NT):
                last = V.bn_aggr(mv[:, n, :], stats[:, n, :])
            link(last)
            link(V.tensor_scalar(var[:, :], mv[:, :, 1], EPS, None, ALU.add))
            link(V.tensor_scalar(rbits[:, :], var[:, :].bitcast(I32), 1, None, ALU.logical_shift_right))
            link(V.tensor_scalar(rs[:, 0, :].bitcast(I32), rbits[:, :], -1.0, float(0x5F3759DF), ALU.mult, ALU.add))
            for i in range(3):
                y, z = rs[:, i % 2, :], rs[:, 1 - i % 2, :]
                link(V.tensor_tensor(rtmp[:, 0, :], y, y, ALU.mult))
                link(V.scalar_tensor_tensor(rtmp[:, 1, :], rtmp[:, 0, :], -0.5, var[:, :], ALU.mult, ALU.mult))
                link(V.scalar_tensor_tensor(z, rtmp[:, 1, :], 1.5, y, ALU.add, ALU.mult))
            wait(dve, rows_rdy, b)
            for n in range(NT):
                last = V.tensor_scalar(xn[:, n, :], xin[:, n, :], mv[:, n, 0:1], rs[:, 1, n:n + 1],
                                       ALU.subtract, ALU.mult)
            last.then_inc(xn_rdy, 1)

        def stage_a_lo(b):
            for k in range(KT):
                dve.wait_ge(xth_rdy, 2 * b + k + 1)
                V.tensor_tensor(xTl[:, k, :], WK[k][:, :], f32(xTh[:, k, :]), ALU.subtract).then_inc(xtl_rdy, 1)
            for i, (bk, hi, lo, g) in enumerate(((1, kdh, kdl, 0), (0, kdh, kdl, 1), (1, qdh, qdl, 0), (0, qdh, qdl, 1))):
                dve.wait_ge(qkh_rdy, 4 * b + i + 1)
                V.tensor_tensor(lo[:, g, :], WK[bk][:, :], f32(hi[:, g, :]), ALU.subtract).then_inc(qkl_rdy, 1)

        def route(b):
            dve.wait_ge(lraw_rdy, NT * b + NT)
            link(V.tensor_tensor(lg[:, :, :], lraw[:, :, :], br_bc[:, :, :], ALU.add))
            V.tensor_copy(cum[:, 0, :], cum[:, NT, :])
            for n in range(NT):
                last = V.max(top8[:, n, :], lg[:, n, :])
            link(last)
            V.tensor_tensor(dlt[:, :, :], lg[:, :, :], top8[:, :, 0:1].to_broadcast([P, NT, E]), ALU.subtract).then_inc(dlt_rdy, 1)
            link(V.tensor_tensor(msk[:, :, :], lg[:, :, :], top8[:, :, 1:2].to_broadcast([P, NT, E]), ALU.is_ge))
            V.tensor_copy(mskb[:, :, :], msk[:, :, :])
            for n in range(NT):
                link(V.tensor_tensor(cum[:, n + 1, :], cum[:, n, :], msk[:, n, :], ALU.add))
            V.tensor_copy(cumb[:, :, :], cum[:, 0:NT, :]).then_inc(mask_rdy, 1)
            dve.wait_ge(ex_rdy, b + 1)
            link(V.tensor_tensor(exm[:, :, :], ex[:, :, :], msk[:, :, :], ALU.mult))
            link(V.tensor_reduce(esum[:, :], exm[:, :, :], AX_X, ALU.add))
            link(V.reciprocal(erec[:, :], esum[:, :]))

        def slots_of(b):
            dve.wait_ge(pos_full, b + 1)
            V.tensor_tensor(slotf[:, 0, :], WK[1][:, 0:NT * E], cst[:, C_SLOT:C_SLOT + NT * E], ALU.add).then_inc(pos_read, 1)
            dve.wait_ge(pos_read, b + 1)
            link(V.tensor_tensor(slotf[:, 1, :], slotf[:, 0, :], msk[:, :, :].rearrange("p n e -> p (n e)"), ALU.mult))
            wait(dve, sent, SENT_INC * b)
            V.tensor_tensor(rows[:, :, W_COL:W_COL + E], exm[:, :, :],
                            erec[:, :].unsqueeze(2).to_broadcast([P, NT, E]), ALU.mult)
            V.tensor_copy(rows[:, :, TOK_COL], tokens[:, :])
            V.tensor_scalar(slots[:, :], slotf[:, 1, :], float(SKIP), None, ALU.add).then_inc(slot_rdy, 1)

        def features(b, u):
            f = 32 * b + u
            dve.wait_ge(exp_done, f + 1)
            if u < 16:
                n, c = u // 4, u % 4
                dst = kp[:, n % 2, c * 512:(c + 1) * 512]
                if c == 0:
                    wait(dve, kv_done, NT * b + n - 1)
            else:
                h = u - 16
                dst = qp[:, h, :]
                if h % 8 == 0:
                    wait(dve, attn_done, 2 * b + h // 8 - 1)
            V.tensor_tensor(dst, e_ring[:, u % 4, :], F[u % 4][:, :], ALU.max).then_inc(feat, 1)

        def denominators(b):
            dve.wait_ge(attn_done, 2 * b + 2)
            V.tensor_scalar(den_sb[:, :], DEN[:, :], 1e-8, None, ALU.add).then_inc(den_read, 1)
            dve.wait_ge(den_read, b + 1)
            V.reciprocal(rec_sb[:, :], den_sb[:, :]).then_inc(rec_rdy, 1)

        def normalise(b):
            for g in range(2):
                dve.wait_ge(num_rdy, 2 * b + g + 1)
                dve.wait_ge(spread_full, 2 * b + g + 1)
                V.tensor_tensor(at[:, g, :], num_sb[:, g, :], WK[g][:, :], ALU.mult).then_inc(at_rdy, 1)

        def at_lo(b):
            for g in range(2):
                dve.wait_ge(ath_rdy, 2 * b + g + 1)
                V.tensor_tensor(atl[:, g, :], at[:, g, :], f32(ath[:, g, :]), ALU.subtract).then_inc(atl_rdy, 1)

        def residual(b):
            dve.wait_ge(xres_rdy, b + 1)
            wait(dve, acc_st, 16 * b)
            for i in range(2):
                dve.wait_ge(proj_full, 2 * b + i + 1)
                V.tensor_tensor(o_sb[:, 2 * i:2 * i + 2, :], WK[i][:, :].rearrange("p (n d) -> p n d", d=D),
                                xres[:, 2 * i:2 * i + 2, :], ALU.add).then_inc(o_rdy, 1)

        def iteration(b, first=False, last=False):
            for u in range(4):
                features(b, u)
            if not first:
                denominators(b - 1)
            for u in range(4, 12):
                features(b, u)
            if not first:
                normalise(b - 1)
            for u in range(12, 16):
                features(b, u)
            if not first:
                at_lo(b - 1)
                residual(b - 1)
            if last:
                V.tensor_copy(totb[:, :], cum[:, NT, :]).then_inc(tot_rdy, 1)
                for u in range(16, 32):
                    features(b, u)
                return
            norm(b + 1)
            stage_a_lo(b + 1)
            for u in range(16, 18):
                features(b, u)
            route(b + 1)
            for u in range(18, 28):
                features(b, u)
            slots_of(b + 1)
            for u in range(28, 32):
                features(b, u)

        chain[:] = setup_steps, 0
        norm(0)
        stage_a_lo(0)
        route(0)
        slots_of(0)
        batch_steps = chain[1]
        chain[:] = setup_steps + batch_steps, 0
        iteration(0, first=True)
        assert chain[1] == batch_steps
        with dve.Fori(1, NB - 1) as b:
            chain[:] = setup_steps + (b + 1) * batch_steps, 0
            iteration(b)
        assert chain[1] == batch_steps
        chain[:] = setup_steps + NB * batch_steps, 0
        iteration(NB - 1, last=True)
        dve.wait_ge(pos_full, NB + 1)
        cnt, tiles_, first_ = counts[0:1, 0, 0:E], counts[0:1, 1, 0:E], counts[0:1, 2, :]
        V.tensor_copy(cnt, WK[1][0:1, 0:E]).then_inc(pos_read, 1)
        dve.wait_ge(pos_read, NB + 1)
        V.tensor_copy(counts_i[0:1, 0, 0:E], cnt)
        link(V.tensor_scalar(counts_i[0:1, 2, 0:E], cnt, float(T - 1), None, ALU.add))
        link(V.tensor_scalar(counts_i[0:1, 3, 0:E], counts_i[0:1, 2, 0:E], T.bit_length() - 1, None, ALU.logical_shift_right))
        link(V.tensor_scalar(tiles_, counts_i[0:1, 3, 0:E], 1.0, None, ALU.max))
        for e in range(E):
            link(V.tensor_tensor(first_[:, e + 1:e + 2], first_[:, e:e + 1], tiles_[:, e:e + 1], ALU.add))
        V.tensor_copy(counts_i[0:1, 1, 0:E + 1], first_[:, 0:E + 1]).then_inc(route_rdy, 1)
        denominators(NB - 1)
        normalise(NB - 1)
        at_lo(NB - 1)
        residual(NB - 1)

        def split_weights(e, w):
            dve.wait_ge(raw_ld, 32 * e + 32)
            V.tensor_copy(wh[w][:, :], wraw[:, :]).then_inc(step, 1)
            V.tensor_copy(b1c[:, w, :], b1T[:, bass.ds(e * MT, MT)])
            dve.wait_ge(step, split_from + e + 1)
            V.tensor_tensor(wl[w][:, :], wraw[:, :], f32(wh[w][:, :]), ALU.subtract).then_inc(w_rdy, 1)

        split_from = chain[0] + chain[1]

        def rows_lo(g):
            dve.wait_ge(grow_ld, 16 * g + 16)
            V.tensor_copy(wnext[:, :, :], grow[:, :, W_COL:W_COL + E])
            V.tensor_copy(inext[:, :], grow[:, :, TOK_COL])
            dve.wait_ge(gxh_rdy, g + 1)
            V.tensor_tensor(gxl[:, :, :], WK[0][:, :].rearrange("p (k t) -> p k t", k=KT),
                            f32(gxh[:, :, :]), ALU.subtract).then_inc(grow_free, 1)

        def tile(g, e):
            for q in range(MT // 2):
                dve.wait_ge(hh_rdy, 4 * g + q + 1)
                V.tensor_tensor(hl[:, 2 * q:2 * q + 2, :], h32[:, 2 * q:2 * q + 2, :],
                                f32(hh[:, 2 * q:2 * q + 2, :]), ALU.subtract).then_inc(hl_rdy, 1)
            dve.wait_ge(sums, SUB * g + SUB)
            V.tensor_copy(wcur[:, :, :], wnext[:, :, bass.ds(e, 1)])
            V.tensor_copy(icur[:, :, 0], inext[:, :]).then_inc(gx_cur, 1)
            dve.wait_ge(gx_cur, g + 1)
            rows_lo(g + 1)
            for s in range(SUB):
                dve.wait_ge(y_full, SUB + SUB * g + s + 1)
                V.tensor_tensor(ytmp[:, s, :], (NUM, DEN)[s][:, 0:D], b2bc[:, bass.ds(e * D, D)], ALU.add).then_inc(y_read, 1)
                dve.wait_ge(y_read, SUB + SUB * g + s + 1)
                V.tensor_scalar(ysb[:, s, :], ytmp[:, s, :], wcur[:, s, :], None, ALU.mult).then_inc(y_rdy, 1)

        dve.wait_ge(f_full, 32 * NB)
        dve.sem_inc(hl_rdy, 4)
        dve.sem_inc(grow_free, 1)
        dve.wait_ge(pad_st, 16)
        dve.wait_ge(o_rdy, 2 * NB)
        dve.sem_inc(y_read, SUB)
        split_weights(0, 0)
        rows_lo(0)
        def expert(e, w, split_next=True):
            lo = dve.value_load(counts_i[0:1, 1, bass.ds(e, 1)], min_val=0, max_val=E * TOKENS // T)
            hi = dve.value_load(counts_i[0:1, 1, bass.ds(e + 1, 1)], min_val=1, max_val=E * TOKENS // T)
            if split_next:
                dve.wait_ge(y_full, SUB + SUB * lo)
                split_weights(e + 1, 1 - w)
            with dve.Fori(lo, hi) as g:
                tile(g, e)

        with dve.Fori(0, E // 2 - 1) as i:
            expert(2 * i, 0)
            expert(2 * i + 1, 1)
        expert(E - 2, 0)
        expert(E - 1, 1, split_next=False)

    @block.gpsimd
    def _(pool):
        last_row = pool.to_reg(E * CAP - 1)
        last_token = pool.to_reg(TOKENS + T - 1)
        batches = pool.alloc_register("batches")
        pool.reg_mov(batches, 1)

        def add_bias(b):
            pool.wait_ge(xres_ld, 16 * b + 32)
            nc.gpsimd.tensor_tensor(xres[:, :, :], xres[:, :, :],
                                    bo_bc[:, :].unsqueeze(1).to_broadcast([P, NT, D]), ALU.add).then_inc(xres_rdy, 1)

        def send(b):
            pool.wait_ge(rows_rdy, b + 1)
            pool.wait_ge(slot_rdy, batches)
            pool.reg_add(batches, batches, 1)
            for n in range(NT):
                for e in range(E):
                    k = n * E + e
                    pool.indirect_dma_start(xg, bass.IndirectOffsetOnAxis(slots[:, k:k + 1], 0), rows[:, n, :], None,
                                            bounds_check=last_row, oob_is_err=False).then_inc(sent, 16)

        send(0)
        add_bias(0)
        send(1)
        with pool.Fori(1, NB - 1) as b:
            add_bias(b)
            send(b + 1)
        add_bias(NB - 1)

        pool.wait_ge(route_rdy, 1)
        total = pool.value_load(counts_i[0:1, 1, E:E + 1], min_val=E, max_val=E * TOKENS // T)
        pool.wait_ge(acc_st, 16 * NB)
        pool.wait_ge(pad_st, 16 * (E + 2))
        pool.sem_inc(sums, SUB)
        parts = pool.alloc_register("parts")
        pool.reg_mov(parts, 1)
        with pool.Fori(0, total) as g:
            for s in range(SUB):
                pool.wait_ge(y_rdy, parts)
                pool.reg_add(parts, parts, 1)
                pool.indirect_dma_start(acc, bass.IndirectOffsetOnAxis(icur[:, s, :], 0), ysb[:, s, :], None,
                                        bounds_check=last_token, compute_op=ALU.add).then_inc(added, 16)
                pool.wait_ge(added, 32 * g + 16 * (s + 1))
                pool.sem_inc(sums, 1)

    block_ctx.__exit__(None, None, None)


INPUTS = ["L0_attn_x", "L0_attn_W_qkv", "L0_attn_proj", "L0_attn_W_out", "L0_attn_b_out", "L0_ffn_W1",
          "L0_ffn_b1", "L0_ffn_W2", "L0_ffn_b2", "L0_ffn_Wr", "L0_ffn_br"]


def kernel(**inputs):
    import numpy as np
    import concourse.bacc as bacc
    from concourse import mybir as _mybir
    from concourse.bass_utils import run_bass_kernel_spmd

    nc = bacc.Bacc("TRN2", target_bir_lowering=False, num_devices=1)
    arrays = {name: np.ascontiguousarray(inputs[name]) for name in INPUTS}
    arrays["constants"] = constants()
    args = [nc.dram_tensor(n, a.shape, _mybir.dt.from_np(a.dtype), kind="ExternalInput").ap() for n, a in arrays.items()]
    out = nc.dram_tensor("out", (NB, NTOK, D), F32, kind="ExternalOutput").ap()
    build(nc, *args, out)
    result = run_bass_kernel_spmd(nc, [arrays], core_ids=[0])
    return result.results[0]["out"]
```

```python
import concourse.bass as bass
from concourse import mybir

F32 = mybir.dt.float32
F32R = mybir.dt.float32r
BF16 = mybir.dt.bfloat16
I32 = mybir.dt.int32
U32 = mybir.dt.uint32
ACT = mybir.ActivationFunctionType
ALU = mybir.AluOpType
AX_X = mybir.AxisListType.X

P = 128
NB, NTOK, D = 8, 512, 256
TOKENS = NB * NTOK
HEADS, HD, FEAT = 16, 16, 128
KT = D // P
NT = NTOK // P
E, HID = 8, 1024
MT = HID // P
T = 256
SUB = T // P
CAP = TOKENS + T
ROWW = 272
W_COL, TOK_COL = D, D + E
SKIP = E * CAP
EPS = 1e-5
QKVR = 3 * D + E
PAIRS = HEADS // 2
SROWS = 97

C_ID, C_TRI, C_SLOT, C_TOK, C_PAD, C_SEL = 0, 128, 256, 288, 320, 324
C_END = C_SEL + 256


def constants():
    import numpy as np
    c = np.zeros((P, C_END), np.float32)
    p = np.arange(P)
    c[:, C_ID:C_ID + P] = np.eye(P)
    c[:, C_TRI:C_TRI + P] = p[:, None] < p[None, :]
    c[:, C_SLOT:C_SLOT + NT * E] = np.tile(np.arange(E) * CAP - SKIP, NT)
    c[:, C_TOK:C_TOK + NB * NT] = p[:, None] + P * np.arange(NB * NT)
    c[:, C_PAD:C_PAD + SUB] = p[:, None] + P * np.arange(SUB) + TOKENS
    for g in range(2):
        for r in range(P):
            c[32 * (r // 32) + 2 * g + (r % 32) // 16, C_SEL + P * g + r] = 1.0
    return c


def build(nc, x, W_qkv, proj, W_out, b_out, W1, b1, W2, b2, Wr, br, consts, out):
    xg = nc.dram_tensor("xg", (E * CAP, ROWW), F32, kind="Internal").ap()
    acc = nc.dram_tensor("acc", (TOKENS + T, D), F32, kind="Internal").ap()
    x_rows = x.rearrange("b (t p) d -> b p t d", p=P)
    acc_rows = acc[0:TOKENS, :].rearrange("(b t p) d -> b p t d", t=NT, p=P)

    place = [nc.sbuf_base + 63 & ~63]

    def sb_at(name, shape, dt, offset):
        return nc.alloc_sbuf_tensor_at(name, shape, dt, offset=offset)

    def sb(name, shape, dt):
        n = 2 if dt == BF16 else 4
        for s in shape[1:]:
            n *= s
        at = place[0]
        place[0] += (n + 63) // 64 * 64
        assert place[0] <= nc.sbuf_usable_end, (name, place[0])
        return sb_at(name, shape, dt, at)

    cst = sb("cst", [P, C_END], F32)
    ident = cst[:, C_ID:C_ID + P]
    tri = sb("tri", [P, P], BF16)
    ones = sb("ones", [P, P], BF16)
    zrows = sb("zrows", [P, SUB, ROWW], F32)
    b1T = sb("b1T", [P, E * MT], F32)
    b2bc = sb("b2bc", [P, E * D], F32)
    counts = sb("counts", [1, 8, 16], F32)
    counts_i = sb("counts_i", [1, 4, 16], I32)
    WTh = sb("WTh", [P, KT, QKVR], F32R)
    WTl = sb("WTl", [P, KT, QKVR], F32R)
    WOh = sb("WOh", [P, KT, D], F32R)
    WOl = sb("WOl", [P, KT, D], F32R)
    stacked_proj = sb("stacked_proj", [P, HEADS, FEAT], F32R)
    br_bc = sb("br_bc", [P, NT, E], F32)
    bo_bc = sb("bo_bc", [P, D], F32)
    xin = sb("xin", [P, NT, D], F32)
    xres = sb("xres", [P, NT, D], F32)
    xn = sb("xn", [P, NT, D], F32)
    rows = sb("rows", [P, NT, ROWW], F32)
    stats = sb("stats", [P, NT, 6], F32)
    mv = sb("mv", [P, NT, 2], F32)
    tokens = sb("tokens", [P, NT], F32)
    var = sb("var", [P, NT], F32)
    rs = sb("rs", [P, 2, NT], F32)
    rtmp = sb("rtmp", [P, 2, NT], F32)
    rbits = sb("rbits", [P, NT], I32)
    lraw = sb("lraw", [P, NT, E], F32)
    lg = sb("lg", [P, NT, E], F32)
    top8 = sb("top8", [P, NT, 8], F32)
    msk = sb("msk", [P, NT, E], F32)
    mskb = sb("mskb", [P, NT, E], BF16)
    dlt = sb("dlt", [P, NT, E], F32)
    ex = sb("ex", [P, NT, E], F32)
    exm = sb("exm", [P, NT, E], F32)
    esum = sb("esum", [P, NT], F32)
    erec = sb("erec", [P, NT], F32)
    cum = sb("cum", [P, NT + 1, E], F32)
    cumb = sb("cumb", [P, NT, E], BF16)
    totb = sb("totb", [P, E], BF16)
    slotf = sb("slotf", [P, 2, NT * E], F32)
    slots = sb("slots", [P, NT * E], U32)
    e_ring = sb("e_ring", [P, 4, 512], F32)
    kv_sb = sb("kv_sb", [P, 512], F32)
    num_w = sb("num_w", [P, HEADS, 32], F32)
    den_w = sb("den_w", [P, HEADS, 32], F32)
    r_num = place[0]
    num_sb = sb("num_sb", [P, 2, 512], F32)
    den_sb = sb("den_sb", [P, 512], F32)
    rec_sb = sb("rec_sb", [P, 512], F32)
    at = sb("at", [P, 2, 512], F32)
    ath = sb("ath", [P, 2, 512], F32R)
    atl = sb("atl", [P, 2, 512], F32R)
    o_sb = sb("o_sb", [P, NT, D], F32)
    r_qp = place[0]
    qp = sb("qp", [P, HEADS, 512], F32)
    r_kp = place[0]
    kp = sb("kp", [P, 2, 2048], F32)
    vext = sb("vext", [P, NT, HEADS, 32], F32)
    kdh = sb("kdh", [P, 2, 512], F32R)
    kdl = sb("kdl", [P, 2, 512], F32R)
    r_xt = place[0]
    xTh = sb("xTh", [P, KT, 512], F32R)
    xTl = sb("xTl", [P, KT, 512], F32R)
    r_sk = place[0]
    Sk = sb("Sk", [P, PAIRS, 512], F32R)
    r_qd = place[0]
    qdh = sb("qdh", [P, 2, 512], F32R)
    qdl = sb("qdl", [P, 2, 512], F32R)
    Sq = sb("Sq", [P, PAIRS, 512], F32R)
    wnat = sb_at("wnat", [P, 8, D], F32, r_qp)
    wr_nat = sb_at("wr_nat", [P, KT, E], F32, r_qp + 8192)
    b1nat = sb_at("b1nat", [E * MT, P], F32, r_qp + 8320)
    praw = sb_at("praw", [P, HEADS, FEAT], F32, r_qp + 9216)
    phi = sb_at("phi", [P, HEADS, FEAT], F32R, r_qp + 17408)
    KB = 1024
    wh = [sb_at("wh0", [P, 4096], F32R, r_kp), sb_at("wh1", [P, 4096], F32R, r_qp)]
    wl = [sb_at("wl0", [P, 4096], F32R, r_kp + 16 * KB), sb_at("wl1", [P, 4096], F32R, r_qp + 16 * KB)]
    wraw = sb_at("wraw", [P, 4096], F32, r_sk)
    gxh = sb_at("gxh", [P, KT, T], F32R, r_xt)
    gxl = sb_at("gxl", [P, KT, T], F32R, r_xt + 2 * KB)
    grow = sb_at("grow", [P, SUB, ROWW], F32, r_xt + 4 * KB)
    h32 = sb_at("h32", [P, MT, T], F32, r_qd)
    hh = sb_at("hh", [P, MT, T], F32R, r_qd + 8 * KB)
    hl = sb_at("hl", [P, MT, T], F32R, r_qd + 16 * KB)
    assert r_xt - r_kp >= 32 * KB and r_sk - r_xt >= 4 * KB + SUB * ROWW * 4 and r_qd - r_sk >= 16 * KB
    place[0] = r_xt + 4 * KB + SUB * ROWW * 4
    b1c = sb("b1c", [P, 2, MT], F32)
    wnext = sb("wnext", [P, SUB, E], F32)
    wcur = sb("wcur", [P, SUB, 1], F32)
    inext = sb("inext", [P, SUB], U32)
    icur = sb("icur", [P, SUB, 1], U32)
    assert place[0] <= r_sk
    ytmp = sb_at("ytmp", [P, SUB, D], F32, r_num)
    ysb = sb_at("ysb", [P, SUB, D], F32, r_num + 2 * KB)

    def bank(name):
        return nc.alloc_psum_tensor(name, [P, 512], F32)

    F = [bank(f"F{i}") for i in range(4)]
    WK = [bank(f"WK{i}") for i in range(2)]
    NUM, DEN = bank("NUM"), bank("DEN")
    QK_BANK = [WK[0], WK[1], NUM, WK[0]]
    V_BANK = [WK[0], WK[1], NUM, WK[0]]
    SPREAD_BANK = [WK[1], NUM]
    PROJ_BANK = [NUM, WK[0]]
    STATE, POS = WK[1], WK[1]
    KV = DEN

    sem = nc.alloc_semaphore
    s_w = sem("s_w")
    s_zero = sem("s_zero")
    s_fill = sem("s_fill")
    s_praw = sem("s_praw")
    s_wT = sem("s_wT")
    s_wTh = sem("s_wTh")
    s_setup = sem("s_setup")
    x_ld = sem("x_ld")
    xres_ld = sem("xres_ld")
    xn_rdy = sem("xn_rdy")
    xT_full = sem("xT_full")
    qk_full = sem("qk_full")
    v_full = sem("v_full")
    pos_full = sem("pos_full")
    pos_read = sem("pos_read")
    state_full = sem("state_full")
    spread_full = sem("spread_full")
    proj_full = sem("proj_full")
    f_full = sem("f_full")
    relu_done = sem("relu_done")
    exp_done = sem("exp_done")
    feat = sem("feat")
    kv_done = sem("kv_done")
    kv_rdy = sem("kv_rdy")
    state_rdy = sem("state_rdy")
    attn_done = sem("attn_done")
    num_rdy = sem("num_rdy")
    den_read = sem("den_read")
    rec_rdy = sem("rec_rdy")
    at_rdy = sem("at_rdy")
    ath_rdy = sem("ath_rdy")
    atl_rdy = sem("atl_rdy")
    xth_rdy = sem("xth_rdy")
    xtl_rdy = sem("xtl_rdy")
    qkh_rdy = sem("qkh_rdy")
    qkl_rdy = sem("qkl_rdy")
    sk_ld = sem("sk_ld")
    sq_ld = sem("sq_ld")
    lraw_rdy = sem("lraw_rdy")
    v_rdy = sem("v_rdy")
    dlt_rdy = sem("dlt_rdy")
    ex_rdy = sem("ex_rdy")
    mask_rdy = sem("mask_rdy")
    rows_rdy = sem("rows_rdy")
    slot_rdy = sem("slot_rdy")
    sent = sem("sent")
    xres_rdy = sem("xres_rdy")
    o_rdy = sem("o_rdy")
    acc_st = sem("acc_st")
    tot_rdy = sem("tot_rdy")
    route_rdy = sem("route_rdy")
    step = sem("step")
    pad_st = sem("pad_st")
    raw_ld = sem("raw_ld")
    w_rdy = sem("w_rdy")
    grow_ld = sem("grow_ld")
    grow_free = sem("grow_free")
    gx_full = sem("gx_full")
    gxh_rdy = sem("gxh_rdy")
    h_full = sem("h_full")
    gelu = sem("gelu")
    hh_rdy = sem("hh_rdy")
    hl_rdy = sem("hl_rdy")
    y_full = sem("y_full")
    y_read = sem("y_read")
    y_rdy = sem("y_rdy")
    added = sem("added")
    sums = sem("sums")
    gx_cur = sem("gx_cur")
    out_st = sem("out_st")

    SETUP_DMAS = 9
    PRAW_DMAS = 6
    STACK_INC = 16 * 12
    SENT_INC = 16 * NT * E
    def wait(eng, s, n):
        if not isinstance(n, int) or n > 0:
            eng.wait_ge(s, n)

    block_ctx = nc.Block()
    block = block_ctx.__enter__()

    @block.sync
    def _(sp):
        sp.dma_start(wnat[:, 0:6, :], W_qkv.rearrange("(c p) d -> p c d", p=P)).then_inc(s_w, 16)
        sp.dma_start(cst[:, :], consts).then_inc(s_w, 16)
        sp.dma_start(xin[:, :, :], x_rows[0]).then_inc(x_ld, 16)
        sp.dma_start(wnat[:, 6:8, :], W_out.rearrange("(c p) d -> p c d", p=P)).then_inc(s_w, 16)
        sp.dma_start(wr_nat[:, :, :], Wr.rearrange("(k p) e -> p k e", p=P)).then_inc(s_w, 16)
        sp.dma_start(b1nat[:, :], b1.rearrange("e (m p) -> (e m) p", p=P)).then_inc(s_w, 16)
        for n in range(NT):
            sp.dma_start(br_bc[:, n, :], br.partition_broadcast(P)).then_inc(s_w, 16)
        sp.wait_ge(s_zero, 1)
        for s in range(2):
            for part in range(3):
                r = 32 * part + 16 * s
                sp.dma_start(praw[r:r + HD, s:HEADS:2, :],
                             proj.rearrange("(i s) d f -> s d i f", s=2)[s]).then_inc(s_praw, 16)
        sp.dma_start(bo_bc[:, :], b_out.partition_broadcast(P)).then_inc(xres_ld, 16)
        sp.dma_start(b2bc[:, :], b2.rearrange("e d -> (e d)").partition_broadcast(P)).then_inc(pad_st, 16)

        def load_x(b):
            wait(sp, xn_rdy, b)
            sp.dma_start(xin[:, :, :], x_rows[b]).then_inc(x_ld, 16)

        def load_xres(b):
            sp.wait_ge(o_rdy, 2 * b + 2)
            sp.dma_start(xres[:, :, :], x_rows[b]).then_inc(xres_ld, 16)

        def stack(dst, hi, lo, done):
            for r in range(4):
                for part, src in enumerate((hi, lo, hi)):
                    sp.dma_start(dst[32 * part:32 * part + 32, r:PAIRS:4, :].bitcast(F32),
                                 src[32 * r:32 * r + 32, :, :].bitcast(F32)).then_inc(done, 16)

        def stack_k(b):
            sp.wait_ge(qkl_rdy, 4 * b + 2)
            wait(sp, f_full, 32 * b - 16)
            stack(Sk, kdh, kdl, sk_ld)

        def stack_q(b):
            sp.wait_ge(qkl_rdy, 4 * b + 4)
            wait(sp, f_full, 32 * b)
            stack(Sq, qdh, qdl, sq_ld)

        def store_o(b):
            sp.wait_ge(o_rdy, 2 * b + 4)
            sp.dma_start(acc_rows[b], o_sb[:, :, :]).then_inc(acc_st, 16)

        load_x(1)
        stack_k(0)
        stack_q(0)
        load_xres(0)
        load_x(2)
        stack_k(1)
        stack_q(1)
        with sp.Fori(1, NB - 2) as b:
            load_x(b + 2)
            stack_k(b + 1)
            store_o(b - 1)
            load_xres(b)
            stack_q(b + 1)
        stack_k(NB - 1)
        store_o(NB - 3)
        load_xres(NB - 2)
        stack_q(NB - 1)
        store_o(NB - 2)
        load_xres(NB - 1)
        def load_raw(e):
            sp.dma_start(wraw[:, 0:2048], W1[e].rearrange("(k p) h -> p k h", p=P)).then_inc(raw_ld, 16)
            sp.dma_start(wraw[:, 2048:4096], W2[e].rearrange("(m p) d -> p m d", p=P)).then_inc(raw_ld, 16)

        sp.wait_ge(f_full, 32 * NB - 16)
        load_raw(0)
        sp.wait_ge(route_rdy, 1)
        for e in range(E):
            n = sp.value_load(counts_i[0:1, 0, e:e + 1], min_val=0, max_val=TOKENS)
            sp.dma_start(xg[bass.ds(n + e * CAP, T), :].rearrange("(s p) c -> p s c", p=P),
                         zrows[:, :, :]).then_inc(pad_st, 16)
        sp.dma_start(acc[TOKENS:TOKENS + T, :].rearrange("(s p) c -> p s c", p=P),
                     zrows[:, :, 0:D]).then_inc(pad_st, 16)
        store_o(NB - 1)
        sp.wait_ge(pad_st, 16 * (E + 2))
        sp.wait_ge(sent, SENT_INC * NB)

        def load_rows(g, first):
            sp.wait_ge(grow_free, g + 1)
            sp.dma_start(grow[:, :, :],
                         xg[bass.ds(first, T), :].rearrange("(s p) c -> p s c", p=P)).then_inc(grow_ld, 16)

        def expert_rows(e):
            lo = sp.value_load(counts_i[0:1, 1, bass.ds(e, 1)], min_val=0, max_val=E * TOKENS // T)
            hi = sp.value_load(counts_i[0:1, 1, bass.ds(e + 1, 1)], min_val=1, max_val=E * TOKENS // T)
            with sp.Fori(lo, hi) as g:
                load_rows(g, nc.s_assert_within((g - lo) * T + e * CAP, 0, E * CAP - T,
                                                skip_runtime_bounds_check_because="a list has at most TOKENS rows"))

        sp.wait_ge(w_rdy, 1)
        load_raw(1)
        with sp.Fori(0, E // 2 - 1) as i:
            for s in range(2):
                expert_rows(2 * i + s)
                sp.wait_ge(w_rdy, 2 * i + s + 2)
                load_raw(2 * i + s + 2)
        expert_rows(E - 2)
        expert_rows(E - 1)
        total = sp.value_load(counts_i[0:1, 1, E:E + 1], min_val=E, max_val=E * TOKENS // T)
        load_rows(total, 0)
        sp.wait_ge(sums, SUB + SUB * total)
        for q in range(4):
            n = TOKENS // 4
            sp.dma_start(out.rearrange("b t d -> (b t) d")[q * n:q * n + n, :],
                         acc[q * n:q * n + n, :]).then_inc(out_st, 16)
        sp.wait_ge(out_st, 64)

    @block.tensor
    def _(pe):
        def mm3(dst, wh_, wl_, mh_, ml_, first, last):
            nc.tensor.matmul(dst, wh_, mh_, start=first, stop=False)
            nc.tensor.matmul(dst, wh_, ml_, start=False, stop=False)
            return nc.tensor.matmul(dst, wl_, mh_, start=False, stop=last)

        pe.wait_ge(s_w, 16 * SETUP_DMAS)
        for k in range(KT):
            for c in range(6):
                t = 6 * k + c
                last = nc.tensor.transpose(F[t // 4][:, t % 4 * P:(t % 4 + 1) * P],
                                           wnat[:, c, k * P:(k + 1) * P], ident)
        last.then_inc(s_wT, 1)
        for k in range(KT):
            for c in range(2):
                last = nc.tensor.transpose(F[3][:, k * D + c * P:k * D + (c + 1) * P],
                                           wnat[:, 6 + c, k * P:(k + 1) * P], ident)
        last.then_inc(s_wT, 1)
        nc.tensor.transpose(NUM[:, 0:E * MT], b1nat[:, :], cst[0:E * MT, C_ID:C_ID + E * MT]).then_inc(s_wT, 1)

        def tokens_T(b, k):
            pe.wait_ge(xn_rdy, b + 1)
            for n in range(NT):
                last = nc.tensor.transpose(WK[k][:, n * P:(n + 1) * P], xn[:, n, k * P:(k + 1) * P], ident)
            last.then_inc(xT_full, 1)

        def qk_group(b, i):
            pe.wait_ge(xtl_rdy, 2 * b + 2)
            col = (D, D + P, 0, P)[i]
            for k in range(KT):
                last = mm3(QK_BANK[i][:, :], WTh[:, k, col:col + P], WTl[:, k, col:col + P],
                           xTh[:, k, :], xTl[:, k, :], k == 0, k == KT - 1)
            last.then_inc(qk_full, 1)

        def v_logits(b, n):
            if n == 0:
                pe.wait_ge(qkl_rdy, 4 * b + 4)
            if n == 3:
                pe.wait_ge(v_rdy, NT * b + 1)
            tok = slice(n * P, (n + 1) * P)
            for k in range(KT):
                last = mm3(V_BANK[n][:, 0:D + E], xTh[:, k, tok], xTl[:, k, tok],
                           WTh[:, k, 2 * D:QKVR], WTl[:, k, 2 * D:QKVR], k == 0, k == KT - 1)
            last.then_inc(v_full, 1)

        def prefix(b):
            pe.wait_ge(mask_rdy, b + 1)
            nc.tensor.matmul(POS[:, 0:NT * E], tri[:, :], mskb[:, :, :], start=True, stop=False)
            nc.tensor.matmul(POS[:, 0:NT * E], ones[:, :], cumb[:, :, :],
                             start=False, stop=True).then_inc(pos_full, 1)

        def unit(b, u):
            wait(pe, feat, 32 * b + u - 3)
            if u < 16:
                if u == 0:
                    pe.wait_ge(sk_ld, STACK_INC * (b + 1))
                n, c = u // 4, u % 4
                for s in range(2):
                    pr = 2 * c + s
                    last = nc.tensor.matmul(F[c][:, s * D:(s + 1) * D], Sk[0:SROWS, pr, n * P:(n + 1) * P],
                                            stacked_proj[0:SROWS, 2 * pr:2 * pr + 2, :], start=True, stop=True)
            else:
                if u == 16:
                    pe.wait_ge(sq_ld, STACK_INC * (b + 1))
                h = u - 16
                last = nc.tensor.matmul(F[h % 4][:, :], stacked_proj[0:SROWS, h, :], Sq[0:SROWS, h // 2, :],
                                        start=True, stop=True)
            last.then_inc(f_full, 1)

        def kv(b, n):
            pe.wait_ge(feat, 32 * b + 4 * n + 4)
            if n == 0:
                pe.wait_ge(v_rdy, NT * b + NT)
                wait(pe, den_read, b)
            for c in range(4):
                for j in range(4):
                    h = 4 * c + j
                    last = nc.tensor.matmul(KV[32 * j:32 * j + 32, c * P:(c + 1) * P], vext[:, n, h, :],
                                            kp[:, n % 2, h * FEAT:(h + 1) * FEAT],
                                            start=n == 0 and c == 0, stop=n == NT - 1, skip_group_check=True)
            last.then_inc(kv_done, 1)

        def state_T(b):
            pe.wait_ge(kv_rdy, b + 1)
            for c in range(4):
                last = nc.tensor.transpose(STATE[:, c * P:(c + 1) * P], kv_sb[:, c * P:(c + 1) * P], ident)
            last.then_inc(state_full, 1)

        def attn(b, g, s):
            if s == 0:
                pe.wait_ge(feat, 32 * b + 16 + 8 * (g + 1))
                pe.wait_ge(state_rdy, b + 1)
                wait(pe, num_rdy, 2 * b + g)
            for j in range(4):
                h = 8 * g + 2 * j + s
                nc.tensor.matmul(NUM[32 * j:32 * j + 32, :], num_w[:, h, :], qp[:, h, :],
                                 start=s == 0, stop=s == 1)
            for j in range(4):
                h = 8 * g + 2 * j + s
                last = nc.tensor.matmul(DEN[32 * j:32 * j + 32, :], den_w[:, h, :], qp[:, h, :],
                                        start=g == 0 and s == 0, stop=g == 1 and s == 1,
                                        skip_group_check=True)
            if s == 1:
                last.then_inc(attn_done, 1)

        def spread(b, g):
            pe.wait_ge(rec_rdy, b + 1)
            nc.tensor.matmul(SPREAD_BANK[g][:, :], cst[:, C_SEL + P * g:C_SEL + P * (g + 1)], rec_sb[:, :],
                             start=True, stop=True).then_inc(spread_full, 1)

        def project(b, i):
            pe.wait_ge(atl_rdy, 2 * b + 2)
            for n in range(2):
                tok = slice((2 * i + n) * P, (2 * i + n + 1) * P)
                for g in range(2):
                    last = mm3(PROJ_BANK[i][:, n * D:(n + 1) * D], ath[:, g, tok], atl[:, g, tok],
                               WOh[:, g, :], WOl[:, g, :], g == 0, g == 1)
            last.then_inc(proj_full, 1)

        def iteration(b, first=False, last=False):
            for u in range(32):
                unit(b, u)
                if u in (3, 4) and not first:
                    attn(b - 1, 1, u - 3)
                if u == 8:
                    kv(b, 0)
                if u == 9 and not last:
                    pe.wait_ge(v_rdy, NT * b + NT)
                    wait(pe, o_rdy, 2 * b)
                    tokens_T(b + 1, 0)
                if u == 10:
                    pe.wait_ge(pos_read, b + 1)
                    if not last:
                        tokens_T(b + 1, 1)
                    else:
                        pe.wait_ge(tot_rdy, 1)
                        nc.tensor.matmul(POS[:, 0:E], ones[:, :], totb[:, :],
                                         start=True, stop=True).then_inc(pos_full, 1)
                if u == 12:
                    kv(b, 1)
                if u == 13 and not last:
                    qk_group(b + 1, 0)
                if u == 14 and not last:
                    qk_group(b + 1, 1)
                if u == 15:
                    if not last:
                        wait(pe, num_rdy, 2 * b)
                        qk_group(b + 1, 2)
                    kv(b, 2)
                if u == 16 and not last:
                    pe.wait_ge(qkl_rdy, 4 * b + 5)
                    qk_group(b + 1, 3)
                if u == 17 and not first:
                    if not last:
                        pe.wait_ge(qkl_rdy, 4 * b + 6)
                    else:
                        pe.wait_ge(pos_read, b + 2)
                    spread(b - 1, 0)
                if u == 18 and not first:
                    if not last:
                        pe.wait_ge(qkl_rdy, 4 * b + 7)
                    else:
                        pe.wait_ge(num_rdy, 2 * b)
                    spread(b - 1, 1)
                if u == 19:
                    kv(b, 3)
                    if not last:
                        v_logits(b + 1, 0)
                if u == 20 and not last:
                    if not first:
                        pe.wait_ge(at_rdy, 2 * b - 1)
                    v_logits(b + 1, 1)
                if u == 21 and not last:
                    if not first:
                        pe.wait_ge(at_rdy, 2 * b)
                    v_logits(b + 1, 2)
                if u == 22 and not last:
                    v_logits(b + 1, 3)
                if u == 23:
                    if not last:
                        pe.wait_ge(v_rdy, NT * b + 6)
                    else:
                        pe.wait_ge(at_rdy, 2 * b - 1)
                    state_T(b)
                if u == 24 and not first:
                    if not last:
                        pe.wait_ge(v_rdy, NT * b + 7)
                    else:
                        pe.wait_ge(at_rdy, 2 * b)
                    project(b - 1, 0)
                if u == 25 and not first:
                    if not last:
                        pe.wait_ge(v_rdy, NT * b + 8)
                    else:
                        pe.wait_ge(o_rdy, 2 * b)
                    project(b - 1, 1)
                if u == 27:
                    if first:
                        pe.wait_ge(v_rdy, NT * b + 7)
                    else:
                        pe.wait_ge(o_rdy, 2 * b + 1)
                if u in (27, 28):
                    attn(b, 0, u - 27)
                if u == 30 and not last:
                    pe.wait_ge(state_rdy, b + 1)
                    prefix(b + 1)

        pe.wait_ge(s_setup, 1)
        for k in range(KT):
            tokens_T(0, k)
        for i in range(4):
            if i == 3:
                pe.wait_ge(qkl_rdy, 1)
            qk_group(0, i)
        for n in range(NT):
            v_logits(0, n)
        pe.wait_ge(v_rdy, 2)
        prefix(0)
        pe.wait_ge(s_fill, 1)
        iteration(0, first=True)
        with pe.Fori(1, NB - 1) as b:
            iteration(b)
        iteration(NB - 1, last=True)
        for s in range(2):
            attn(NB - 1, 1, s)
        pe.wait_ge(state_rdy, NB)
        spread(NB - 1, 0)
        pe.wait_ge(num_rdy, 2 * NB)
        spread(NB - 1, 1)
        pe.wait_ge(at_rdy, 2 * NB)
        project(NB - 1, 0)
        pe.wait_ge(o_rdy, 2 * NB)
        project(NB - 1, 1)

        def rows_T(g):
            pe.wait_ge(grow_ld, 16 * g + 16)
            pe.wait_ge(grow_free, g + 1)
            for k in range(KT):
                for s in range(SUB):
                    last = nc.tensor.transpose(WK[0][:, k * T + s * P:k * T + (s + 1) * P],
                                               grow[:, s, k * P:(k + 1) * P], ident)
            last.then_inc(gx_full, 1)

        def tile(g, w):
            w1 = [wh[w][:, 0:2048].rearrange("p (k h) -> p k h", k=KT), wl[w][:, 0:2048].rearrange("p (k h) -> p k h", k=KT)]
            w2 = [wh[w][:, 2048:4096].rearrange("p (m d) -> p m d", m=MT), wl[w][:, 2048:4096].rearrange("p (m d) -> p m d", m=MT)]
            pe.wait_ge(grow_free, g + 2)
            for m in range(MT):
                pe.wait_ge(gelu, MT * g + m + 1)
                for k in range(KT):
                    hid = slice(m * P, (m + 1) * P)
                    last = mm3(F[m % 4][:, 0:T], w1[0][:, k, hid], w1[1][:, k, hid],
                               gxh[:, k, :], gxl[:, k, :], k == 0, k == KT - 1)
                last.then_inc(h_full, 1)
            rows_T(g + 1)
            for s in range(SUB):
                pe.wait_ge(y_read, SUB * g + s + 1)
                row = slice(s * P, (s + 1) * P)
                for m in range(MT):
                    if s == 0 and m % 2 == 0:
                        pe.wait_ge(hl_rdy, 4 + 4 * g + m // 2 + 1)
                    last = mm3((NUM, DEN)[s][:, 0:D], hh[:, m, row], hl[:, m, row],
                               w2[0][:, m, :], w2[1][:, m, :], m == 0, m == MT - 1)
                last.then_inc(y_full, 1)

        pe.sem_inc(y_full, SUB)
        pe.wait_ge(route_rdy, 1)
        pe.wait_ge(feat, 32 * NB)
        pe.wait_ge(num_rdy, 2 * NB)
        pe.wait_ge(den_read, NB)
        pe.wait_ge(o_rdy, 2 * NB + 2)
        rows_T(0)
        with pe.Fori(0, E // 2) as i:
            for s in range(2):
                lo = pe.value_load(counts_i[0:1, 1, bass.ds(2 * i + s, 1)], min_val=0, max_val=E * TOKENS // T)
                hi = pe.value_load(counts_i[0:1, 1, bass.ds(2 * i + s + 1, 1)], min_val=1, max_val=E * TOKENS // T)
                with pe.Fori(lo, hi) as g:
                    pe.wait_ge(w_rdy, 2 * i + s + 1)
                    tile(g, s)

    @block.scalar
    def _(act):
        A = nc.scalar.activation
        act.wait_ge(s_wT, 1)
        for k in range(KT):
            for c in range(6):
                t = 6 * k + c
                last = A(WTh[:, k, c * P:(c + 1) * P], F[t // 4][:, t % 4 * P:(t % 4 + 1) * P], ACT.Copy)
        last = A(WTh[:, :, 3 * D:QKVR], wr_nat[:, :, :], ACT.Copy)
        act.wait_ge(s_wT, 2)
        A(WOh[:, :, :], F[3][:, :].rearrange("p (k d) -> p k d", k=KT), ACT.Copy).then_inc(s_wTh, 1)
        act.wait_ge(s_praw, 16 * PRAW_DMAS)
        A(phi[64:96, :, :], praw[64:96, :, :], ACT.Copy).then_inc(s_wTh, 1)

        def tokens_hi(b, k):
            act.wait_ge(xT_full, 2 * b + k + 1)
            A(xTh[:, k, :], WK[k][:, :], ACT.Copy).then_inc(xth_rdy, 1)

        def qk_hi(b, i):
            act.wait_ge(qk_full, 4 * b + i + 1)
            if i % 2 == 0:
                wait(act, (sk_ld, sq_ld)[i // 2], STACK_INC * b)
            A((kdh, qdh)[i // 2][:, i % 2, :], QK_BANK[i][:, :], ACT.Copy).then_inc(qkh_rdy, 1)

        def v_copy(b, n):
            act.wait_ge(v_full, NT * b + n + 1)
            if n == 0:
                wait(act, dlt_rdy, b)
            A(lraw[:, n, :], V_BANK[n][:, D:D + E], ACT.Copy).then_inc(lraw_rdy, 1)
            A(vext[:, n, :, 0:HD], V_BANK[n][:, 0:D].rearrange("p (h d) -> p h d", d=HD),
              ACT.Copy).then_inc(v_rdy, 1)

        def route(b):
            act.wait_ge(dlt_rdy, b + 1)
            A(ex[:, :, :], dlt[:, :, :], ACT.Exp).then_inc(ex_rdy, 1)

        def send_rows(b):
            wait(act, sent, SENT_INC * b)
            A(rows[:, :, 0:D], xn[:, :, :], ACT.Copy).then_inc(rows_rdy, 1)

        def relu(b, u):
            f = 32 * b + u
            act.wait_ge(f_full, f + 1)
            wait(act, feat, f - 3)
            A(e_ring[:, u % 4, :], F[u % 4][:, :], ACT.Relu, bias=1.0, scale=-1.0).then_inc(relu_done, 1)

        def exp(b, u):
            act.wait_ge(relu_done, 32 * b + u + 1)
            A(e_ring[:, u % 4, :], e_ring[:, u % 4, :], ACT.Exp, scale=-1.0).then_inc(exp_done, 1)

        def at_hi(b, g):
            act.wait_ge(at_rdy, 2 * b + g + 1)
            A(ath[:, g, :], at[:, g, :], ACT.Copy).then_inc(ath_rdy, 1)

        def copy_num(b, g):
            act.wait_ge(attn_done, 2 * b + g + 1)
            wait(act, at_rdy, 2 * (b - 1) + g + 1)
            A(num_sb[:, g, :], NUM[:, :], ACT.Copy).then_inc(num_rdy, 1)

        def state(b):
            act.wait_ge(state_full, b + 1)
            wait(act, attn_done, 2 * b)
            st = STATE[:, :].rearrange("p (h c) -> p h c", c=32)
            for s in range(2):
                last = A(num_w[:, s:HEADS:2, 16 * s:16 * s + HD], st[:, s:HEADS:2, 0:HD], ACT.Copy)
            for g in range(2):
                for s in range(2):
                    last = A(den_w[:, 8 * g + s:8 * g + 8:2, 2 * g + s:2 * g + s + 1],
                             st[:, 8 * g + s:8 * g + 8:2, HD:HD + 1], ACT.Copy)
            last.then_inc(state_rdy, 1)

        def iteration(b, first=False, last=False):
            relu(b, 0)
            for u in range(32):
                if u < 31:
                    relu(b, u + 1)
                exp(b, u)
                if u == 4 and not first:
                    copy_num(b - 1, 1)
                if u in (8, 9) and not last:
                    tokens_hi(b + 1, u - 8)
                if 12 <= u < 16 and not last:
                    qk_hi(b + 1, u - 12)
                if u in (17, 18) and not first:
                    at_hi(b - 1, u - 17)
                if u == 18:
                    act.wait_ge(kv_done, NT * b + NT)
                    A(kv_sb[:, :], KV[:, :], ACT.Copy).then_inc(kv_rdy, 1)
                if 18 <= u < 22 and not last:
                    v_copy(b + 1, u - 18)
                if u == 22:
                    state(b)
                if u == 26 and not last:
                    route(b + 1)
                if u == 29:
                    copy_num(b, 0)
                if u == 30 and not last:
                    send_rows(b + 1)

        act.wait_ge(s_setup, 1)
        act.wait_ge(s_fill, 1)
        for k in range(KT):
            tokens_hi(0, k)
        for i in range(4):
            qk_hi(0, i)
        for n in range(NT):
            v_copy(0, n)
        route(0)
        send_rows(0)
        iteration(0, first=True)
        with act.Fori(1, NB - 1) as b:
            iteration(b)
        iteration(NB - 1, last=True)
        copy_num(NB - 1, 1)
        for g in range(2):
            at_hi(NB - 1, g)

        def rows_hi(g):
            act.wait_ge(gx_full, g + 1)
            A(gxh[:, :, :], WK[0][:, :].rearrange("p (k t) -> p k t", k=KT), ACT.Copy).then_inc(gxh_rdy, 1)

        def tile(g, w):
            for m in range(MT):
                act.wait_ge(h_full, MT * g + m + 1)
                if m % 2 == 0:
                    act.wait_ge(hl_rdy, 4 * g + m // 2 + 1)
                A(h32[:, m, :], F[m % 4][:, 0:T], ACT.Gelu, bias=b1c[:, w, m:m + 1]).then_inc(gelu, 1)
                if m % 2 == 1:
                    if m == 1:
                        act.wait_ge(y_full, SUB * g + SUB)
                    act.wait_ge(gelu, 4 + MT * g + m + 1)
                    A(hh[:, m - 1:m + 1, :], h32[:, m - 1:m + 1, :], ACT.Copy).then_inc(hh_rdy, 1)
            rows_hi(g + 1)

        A(lg[0:1, 0, :], lraw[0:1, 0, :], ACT.Gelu)
        act.sem_inc(gelu, 4)
        act.wait_ge(route_rdy, 1)
        rows_hi(0)
        with act.Fori(0, E // 2) as i:
            for s in range(2):
                lo = act.value_load(counts_i[0:1, 1, bass.ds(2 * i + s, 1)], min_val=0, max_val=E * TOKENS // T)
                hi = act.value_load(counts_i[0:1, 1, bass.ds(2 * i + s + 1, 1)], min_val=1, max_val=E * TOKENS // T)
                with act.Fori(lo, hi) as g:
                    act.wait_ge(w_rdy, 2 * i + s + 1)
                    tile(g, s)

    @block.vector
    def _(dve):
        V = nc.vector
        chain = [0, 0]

        def link(ins):
            ins.then_inc(step, 1)
            chain[1] += 1

        def join():
            dve.wait_ge(step, chain[0] + chain[1])

        def f32(t):
            return t.bitcast(F32)

        V.memset(cum[:, :, :], 0.0)
        link(V.memset(zrows[:, :, :], 0.0))
        V.memset(ones[:, :], 1.0)
        V.memset(counts[:, :, :], 0.0)
        join()
        dve.wait_ge(s_w, 16 * SETUP_DMAS)
        V.tensor_copy(tri[:, :], cst[:, C_TRI:C_TRI + P])
        V.tensor_copy(zrows[:, :, TOK_COL], cst[:, C_PAD:C_PAD + SUB])
        dve.wait_ge(s_wT, 3)
        V.tensor_copy(b1T[:, :], NUM[:, 0:E * MT])
        dve.wait_ge(s_wTh, 1)
        for k in range(KT):
            for c in range(6):
                t = 6 * k + c
                V.tensor_tensor(WTl[:, k, c * P:(c + 1) * P], F[t // 4][:, t % 4 * P:(t % 4 + 1) * P],
                                f32(WTh[:, k, c * P:(c + 1) * P]), ALU.subtract)
        V.tensor_tensor(WTl[:, :, 3 * D:QKVR], wr_nat[:, :, :], f32(WTh[:, :, 3 * D:QKVR]), ALU.subtract)
        V.tensor_tensor(WOl[:, :, :], F[3][:, :].rearrange("p (k d) -> p k d", k=KT), f32(WOh[:, :, :]), ALU.subtract)
        dve.wait_ge(s_fill, 1)
        dve.wait_ge(s_wTh, 2)
        V.tensor_copy(stacked_proj[0:64, :, :], praw[0:64, :, :])
        V.tensor_tensor(stacked_proj[64:96, :, :], praw[64:96, :, :], f32(phi[64:96, :, :]), ALU.subtract)
        V.tensor_copy(stacked_proj[96:97, :, :], praw[96:97, :, :]).then_inc(s_setup, 1)

        def norm_stats(b, lo, hi):
            dve.wait_ge(x_ld, 16 * b + 16)
            for n in range(lo, hi):
                last = V.bn_stats(stats[:, n, :], xin[:, n, :])
            link(last)

        def norm_var(b):
            join()
            V.tensor_copy(tokens[:, :], cst[:, bass.ds(C_TOK + NT * b, NT)])
            for n in range(NT):
                last = V.bn_aggr(mv[:, n, :], stats[:, n, :])
            link(last)

        def norm_guess(b):
            join()
            link(V.tensor_scalar(var[:, :], mv[:, :, 1], EPS, None, ALU.add))
            join()
            link(V.tensor_scalar(rbits[:, :], var[:, :].bitcast(I32), 1, None, ALU.logical_shift_right))
            join()
            link(V.tensor_scalar(rs[:, 0, :].bitcast(I32), rbits[:, :], -1.0, float(0x5F3759DF), ALU.mult, ALU.add))

        def norm_newton(b, i):
            y, z = rs[:, i % 2, :], rs[:, 1 - i % 2, :]
            join()
            link(V.tensor_tensor(rtmp[:, 0, :], y, y, ALU.mult))
            join()
            link(V.scalar_tensor_tensor(rtmp[:, 1, :], rtmp[:, 0, :], -0.5, var[:, :], ALU.mult, ALU.mult))
            join()
            link(V.scalar_tensor_tensor(z, rtmp[:, 1, :], 1.5, y, ALU.add, ALU.mult))

        def norm_rows(b, lo, hi):
            if lo == 0:
                join()
                wait(dve, rows_rdy, b)
            for n in range(lo, hi):
                last = V.tensor_scalar(xn[:, n, :], xin[:, n, :], mv[:, n, 0:1], rs[:, 1, n:n + 1],
                                       ALU.subtract, ALU.mult)
            if hi == NT:
                last.then_inc(xn_rdy, 1)

        def tokens_lo(b, k):
            dve.wait_ge(xth_rdy, 2 * b + k + 1)
            V.tensor_tensor(xTl[:, k, :], WK[k][:, :], f32(xTh[:, k, :]), ALU.subtract).then_inc(xtl_rdy, 1)

        def qk_lo(b, i):
            hi, lo = ((kdh, kdl), (qdh, qdl))[i // 2]
            dve.wait_ge(qkh_rdy, 4 * b + i + 1)
            V.tensor_tensor(lo[:, i % 2, :], QK_BANK[i][:, :], f32(hi[:, i % 2, :]), ALU.subtract).then_inc(qkl_rdy, 1)

        def route_top(b):
            dve.wait_ge(lraw_rdy, NT * b + NT)
            link(V.tensor_tensor(lg[:, :, :], lraw[:, :, :], br_bc[:, :, :], ALU.add))
            join()
            V.tensor_copy(cum[:, 0, :], cum[:, NT, :])
            for n in range(NT):
                last = V.max(top8[:, n, :], lg[:, n, :])
            link(last)

        def route_mask(b):
            join()
            V.tensor_tensor(dlt[:, :, :], lg[:, :, :], top8[:, :, 0:1].to_broadcast([P, NT, E]), ALU.subtract).then_inc(dlt_rdy, 1)
            link(V.tensor_tensor(msk[:, :, :], lg[:, :, :], top8[:, :, 1:2].to_broadcast([P, NT, E]), ALU.is_ge))
            join()
            V.tensor_copy(mskb[:, :, :], msk[:, :, :])

        def route_count(b):
            for n in range(NT):
                link(V.tensor_tensor(cum[:, n + 1, :], cum[:, n, :], msk[:, n, :], ALU.add))
                join()
            V.tensor_copy(cumb[:, :, :], cum[:, 0:NT, :]).then_inc(mask_rdy, 1)

        def route_weights(b):
            dve.wait_ge(ex_rdy, b + 1)
            link(V.tensor_tensor(exm[:, :, :], ex[:, :, :], msk[:, :, :], ALU.mult))
            join()
            link(V.tensor_reduce(esum[:, :], exm[:, :, :], AX_X, ALU.add))
            join()
            link(V.reciprocal(erec[:, :], esum[:, :]))

        def slots_of(b):
            dve.wait_ge(pos_full, b + 1)
            V.tensor_tensor(slotf[:, 0, :], POS[:, 0:NT * E], cst[:, C_SLOT:C_SLOT + NT * E], ALU.add).then_inc(pos_read, 1)
            dve.wait_ge(pos_read, b + 1)
            join()
            link(V.tensor_tensor(slotf[:, 1, :], slotf[:, 0, :], msk[:, :, :].rearrange("p n e -> p (n e)"), ALU.mult))
            wait(dve, sent, SENT_INC * b)
            V.tensor_tensor(rows[:, :, W_COL:W_COL + E], exm[:, :, :],
                            erec[:, :].unsqueeze(2).to_broadcast([P, NT, E]), ALU.mult)
            link(V.tensor_copy(rows[:, :, TOK_COL], tokens[:, :]))
            join()
            V.tensor_scalar(slots[:, :], slotf[:, 1, :], float(SKIP), None, ALU.add).then_inc(slot_rdy, 1)

        def features(b, u):
            f = 32 * b + u
            dve.wait_ge(exp_done, f + 1)
            if u < 16:
                n, c = u // 4, u % 4
                dst = kp[:, n % 2, c * 512:(c + 1) * 512]
                if c == 0:
                    wait(dve, kv_done, NT * b + n - 1)
            else:
                h = u - 16
                dst = qp[:, h, :]
                if h % 8 == 0:
                    wait(dve, attn_done, 2 * b + h // 8 - 1)
            V.tensor_tensor(dst, e_ring[:, u % 4, :], F[u % 4][:, :], ALU.max).then_inc(feat, 1)

        def denominators(b):
            dve.wait_ge(attn_done, 2 * b + 2)
            V.tensor_scalar(den_sb[:, :], DEN[:, :], 1e-8, None, ALU.add).then_inc(den_read, 1)

        def reciprocals(b, q):
            dve.wait_ge(den_read, b + 1)
            cols = slice(q * P, (q + 1) * P)
            last = V.reciprocal(rec_sb[:, cols], den_sb[:, cols])
            if q == 3:
                last.then_inc(rec_rdy, 1)

        def normalise(b, g):
            dve.wait_ge(num_rdy, 2 * b + g + 1)
            dve.wait_ge(spread_full, 2 * b + g + 1)
            V.tensor_tensor(at[:, g, :], num_sb[:, g, :], SPREAD_BANK[g][:, :], ALU.mult).then_inc(at_rdy, 1)

        def at_lo(b, g):
            dve.wait_ge(ath_rdy, 2 * b + g + 1)
            V.tensor_tensor(atl[:, g, :], at[:, g, :], f32(ath[:, g, :]), ALU.subtract).then_inc(atl_rdy, 1)

        def residual(b, i):
            if i == 0:
                dve.wait_ge(xres_rdy, b + 1)
                wait(dve, acc_st, 16 * b)
            dve.wait_ge(proj_full, 2 * b + i + 1)
            V.tensor_tensor(o_sb[:, 2 * i:2 * i + 2, :], PROJ_BANK[i][:, :].rearrange("p (n d) -> p n d", d=D),
                            xres[:, 2 * i:2 * i + 2, :], ALU.add).then_inc(o_rdy, 1)

        def iteration(b, first=False, last=False):
            for u in range(32):
                features(b, u)
                if not last:
                    if u < 2:
                        norm_stats(b + 1, 2 * u, 2 * u + 2)
                    if u == 2:
                        norm_var(b + 1)
                        norm_guess(b + 1)
                    if u == 3:
                        norm_newton(b + 1, 0)
                        norm_newton(b + 1, 1)
                    if u == 4:
                        norm_newton(b + 1, 2)
                        norm_rows(b + 1, 0, 2)
                    if u == 5:
                        norm_rows(b + 1, 2, 4)
                    if u in (8, 9):
                        tokens_lo(b + 1, u - 8)
                    if 12 <= u < 16:
                        qk_lo(b + 1, u - 12)
                    if u == 22:
                        route_top(b + 1)
                    if u == 25:
                        route_mask(b + 1)
                    if u == 26:
                        route_count(b + 1)
                    if u == 28:
                        route_weights(b + 1)
                    if u == 30:
                        slots_of(b + 1)
                elif u == 0:
                    V.tensor_copy(totb[:, :], cum[:, NT, :]).then_inc(tot_rdy, 1)
                elif u == 12:
                    token_counts()
                if not first:
                    if u == 5:
                        denominators(b - 1)
                    if u in (6, 7, 10, 11):
                        reciprocals(b - 1, (6, 7, 10, 11).index(u))
                    if u in (16, 17):
                        normalise(b - 1, u - 16)
                    if u in (18, 19):
                        at_lo(b - 1, u - 18)
                    if u in (23, 24):
                        residual(b - 1, u - 23)

        def token_counts():
            dve.wait_ge(pos_full, NB + 1)
            cnt, tiles_, first_ = counts[0:1, 0, 0:E], counts[0:1, 1, 0:E], counts[0:1, 2, :]
            V.tensor_copy(cnt, POS[0:1, 0:E]).then_inc(pos_read, 1)
            dve.wait_ge(pos_read, NB + 1)
            V.tensor_copy(counts_i[0:1, 0, 0:E], cnt)
            link(V.tensor_scalar(counts_i[0:1, 2, 0:E], cnt, float(T - 1), None, ALU.add))
            join()
            link(V.tensor_scalar(counts_i[0:1, 3, 0:E], counts_i[0:1, 2, 0:E], T.bit_length() - 1, None, ALU.logical_shift_right))
            join()
            link(V.tensor_scalar(tiles_, counts_i[0:1, 3, 0:E], 1.0, None, ALU.max))
            for e in range(E):
                join()
                link(V.tensor_tensor(first_[:, e + 1:e + 2], first_[:, e:e + 1], tiles_[:, e:e + 1], ALU.add))
            join()
            V.tensor_copy(counts_i[0:1, 1, 0:E + 1], first_[:, 0:E + 1]).then_inc(route_rdy, 1)

        dve.sem_inc(o_rdy, 2)
        norm_stats(0, 0, NT)
        norm_var(0)
        norm_guess(0)
        for i in range(3):
            norm_newton(0, i)
        norm_rows(0, 0, NT)
        for k in range(KT):
            tokens_lo(0, k)
        for i in range(4):
            qk_lo(0, i)
        route_top(0)
        route_mask(0)
        route_count(0)
        route_weights(0)
        slots_of(0)
        before = chain[1]
        chain[:] = before, 0
        iteration(0, first=True)
        batch_steps = chain[1]
        with dve.Fori(1, NB - 1) as b:
            chain[:] = before + b * batch_steps, 0
            iteration(b)
        assert chain[1] == batch_steps
        chain[:] = before + (NB - 1) * batch_steps, 0
        iteration(NB - 1, last=True)
        denominators(NB - 1)
        for q in range(4):
            reciprocals(NB - 1, q)
        for g in range(2):
            normalise(NB - 1, g)
        for g in range(2):
            at_lo(NB - 1, g)
        for i in range(2):
            residual(NB - 1, i)

        def split_weights(e, w):
            dve.wait_ge(raw_ld, 32 * e + 32)
            V.tensor_copy(wh[w][:, :], wraw[:, :]).then_inc(step, 1)
            V.tensor_copy(b1c[:, w, :], b1T[:, bass.ds(e * MT, MT)])
            dve.wait_ge(step, split_from + e + 1)
            V.tensor_tensor(wl[w][:, :], wraw[:, :], f32(wh[w][:, :]), ALU.subtract).then_inc(w_rdy, 1)

        split_from = chain[0] + chain[1]

        def rows_lo(g):
            dve.wait_ge(grow_ld, 16 * g + 16)
            V.tensor_copy(wnext[:, :, :], grow[:, :, W_COL:W_COL + E])
            V.tensor_copy(inext[:, :], grow[:, :, TOK_COL])
            dve.wait_ge(gxh_rdy, g + 1)
            V.tensor_tensor(gxl[:, :, :], WK[0][:, :].rearrange("p (k t) -> p k t", k=KT),
                            f32(gxh[:, :, :]), ALU.subtract).then_inc(grow_free, 1)

        def tile(g, e):
            for q in range(MT // 2):
                dve.wait_ge(hh_rdy, 4 * g + q + 1)
                V.tensor_tensor(hl[:, 2 * q:2 * q + 2, :], h32[:, 2 * q:2 * q + 2, :],
                                f32(hh[:, 2 * q:2 * q + 2, :]), ALU.subtract).then_inc(hl_rdy, 1)
            dve.wait_ge(sums, SUB * g + SUB)
            V.tensor_copy(wcur[:, :, :], wnext[:, :, bass.ds(e, 1)])
            V.tensor_copy(icur[:, :, 0], inext[:, :]).then_inc(gx_cur, 1)
            dve.wait_ge(gx_cur, g + 1)
            rows_lo(g + 1)
            for s in range(SUB):
                dve.wait_ge(y_full, SUB + SUB * g + s + 1)
                V.tensor_tensor(ytmp[:, s, :], (NUM, DEN)[s][:, 0:D], b2bc[:, bass.ds(e * D, D)], ALU.add).then_inc(y_read, 1)
                dve.wait_ge(y_read, SUB + SUB * g + s + 1)
                V.tensor_scalar(ysb[:, s, :], ytmp[:, s, :], wcur[:, s, :], None, ALU.mult).then_inc(y_rdy, 1)

        dve.wait_ge(f_full, 32 * NB)
        dve.sem_inc(hl_rdy, 4)
        dve.sem_inc(grow_free, 1)
        dve.wait_ge(pad_st, 16)
        dve.wait_ge(o_rdy, 2 * NB + 2)
        dve.sem_inc(y_read, SUB)
        split_weights(0, 0)
        rows_lo(0)
        def expert(e, w, split_next=True):
            lo = dve.value_load(counts_i[0:1, 1, bass.ds(e, 1)], min_val=0, max_val=E * TOKENS // T)
            hi = dve.value_load(counts_i[0:1, 1, bass.ds(e + 1, 1)], min_val=1, max_val=E * TOKENS // T)
            if split_next:
                dve.wait_ge(y_full, SUB + SUB * lo)
                split_weights(e + 1, 1 - w)
            with dve.Fori(lo, hi) as g:
                tile(g, e)

        with dve.Fori(0, E // 2 - 1) as i:
            expert(2 * i, 0)
            expert(2 * i + 1, 1)
        expert(E - 2, 0)
        expert(E - 1, 1, split_next=False)

    @block.gpsimd
    def _(pool):
        last_row = pool.to_reg(E * CAP - 1)
        last_token = pool.to_reg(TOKENS + T - 1)
        batches = pool.alloc_register("batches")
        pool.reg_mov(batches, 1)

        nc.gpsimd.memset(praw[:, :, :], 0.0).then_inc(s_zero, 1)
        nc.gpsimd.memset(vext[:, :, :, HD:32], 1.0)
        nc.gpsimd.memset(num_w[:, :, :], 0.0)
        nc.gpsimd.memset(den_w[:, :, :], 0.0)
        nc.gpsimd.memset(rows[:, :, TOK_COL:ROWW], 0.0).then_inc(s_zero, 1)
        pool.wait_ge(s_zero, 2)
        nc.gpsimd.memset(Sk[96:97, :, :].bitcast(F32), 1.0)
        nc.gpsimd.memset(Sq[96:97, :, :].bitcast(F32), 1.0)
        pool.wait_ge(s_praw, 16 * PRAW_DMAS)
        nc.gpsimd.memset(praw[96:97, :, :], 1.0).then_inc(s_fill, 1)
        pool.wait_ge(s_fill, 1)

        def add_bias(b):
            pool.wait_ge(xres_ld, 16 * b + 32)
            nc.gpsimd.tensor_tensor(xres[:, :, :], xres[:, :, :],
                                    bo_bc[:, :].unsqueeze(1).to_broadcast([P, NT, D]), ALU.add).then_inc(xres_rdy, 1)

        def send(b, bias_of=None):
            pool.wait_ge(rows_rdy, b + 1)
            pool.wait_ge(slot_rdy, batches)
            pool.reg_add(batches, batches, 1)
            for n in range(NT):
                if n == 2 and bias_of is not None:
                    add_bias(bias_of)
                for e in range(E):
                    k = n * E + e
                    pool.indirect_dma_start(xg, bass.IndirectOffsetOnAxis(slots[:, k:k + 1], 0), rows[:, n, :], None,
                                            bounds_check=last_row, oob_is_err=False).then_inc(sent, 16)

        send(0)
        with pool.Fori(1, NB) as b:
            send(b, b - 1)
        add_bias(NB - 1)

        pool.wait_ge(route_rdy, 1)
        total = pool.value_load(counts_i[0:1, 1, E:E + 1], min_val=E, max_val=E * TOKENS // T)
        pool.wait_ge(acc_st, 16 * NB)
        pool.wait_ge(pad_st, 16 * (E + 2))
        pool.sem_inc(sums, SUB)
        parts = pool.alloc_register("parts")
        pool.reg_mov(parts, 1)
        with pool.Fori(0, total) as g:
            for s in range(SUB):
                pool.wait_ge(y_rdy, parts)
                pool.reg_add(parts, parts, 1)
                pool.indirect_dma_start(acc, bass.IndirectOffsetOnAxis(icur[:, s, :], 0), ysb[:, s, :], None,
                                        bounds_check=last_token, compute_op=ALU.add).then_inc(added, 16)
                pool.wait_ge(added, 32 * g + 16 * (s + 1))
                pool.sem_inc(sums, 1)

    block_ctx.__exit__(None, None, None)


INPUTS = ["L0_attn_x", "L0_attn_W_qkv", "L0_attn_proj", "L0_attn_W_out", "L0_attn_b_out", "L0_ffn_W1",
          "L0_ffn_b1", "L0_ffn_W2", "L0_ffn_b2", "L0_ffn_Wr", "L0_ffn_br"]


def kernel(**inputs):
    import numpy as np
    import concourse.bacc as bacc
    from concourse import mybir as _mybir
    from concourse.bass_utils import run_bass_kernel_spmd

    nc = bacc.Bacc("TRN2", target_bir_lowering=False, num_devices=1)
    arrays = {name: np.ascontiguousarray(inputs[name]) for name in INPUTS}
    arrays["constants"] = constants()
    args = [nc.dram_tensor(n, a.shape, _mybir.dt.from_np(a.dtype), kind="ExternalInput").ap() for n, a in arrays.items()]
    out = nc.dram_tensor("out", (NB, NTOK, D), F32, kind="ExternalOutput").ap()
    build(nc, *args, out)
    result = run_bass_kernel_spmd(nc, [arrays], core_ids=[0])
    return result.results[0]["out"]
```
